# Optimizing a Trainium2 kernel written in Bass

```python
import numpy as np
import jax
import jax.numpy as jnp

def _softmax(x, axis=-1):
    return jax.nn.softmax(x, axis=axis)

def _gelu(x):
    return jax.nn.gelu(x, approximate=True)

def _silu(x):
    return jax.nn.silu(x)

def _sigmoid(x):
    return jax.nn.sigmoid(x)

def _layernorm(x, axis=-1, eps=1e-05):
    m = jnp.mean(x, axis=axis, keepdims=True)
    v = jnp.var(x, axis=axis, keepdims=True)
    return (x - m) / jnp.sqrt(v + eps)

def _scatter_add(tgt, idx, src, axis=0):
    return tgt.at[idx].add(src)

def _segment_sum(src, seg, n):
    return jax.ops.segment_sum(src, seg, n)
kernel_name = 'mk_gnn_resnorm_d2_gnn_r32_d7b6f4'

def setup_inputs(seed: int=0):
    np.random.seed(seed)
    _w = jnp.asarray

    def _rec_inputs():
        import jax
        import jax.numpy as jnp
        _gk = jax.random.key(seed)
        x = -0.0005121 + 1.001 * jax.random.normal(jax.random.fold_in(_gk, 1), (3125, 64), jnp.float32)
        src = jax.random.randint(jax.random.fold_in(_gk, 2), (100000,), 0, 3125, jnp.int32)
        dst = jax.random.randint(jax.random.fold_in(_gk, 3), (100000,), 0, 3125, jnp.int32)
        _o = jnp.argsort(dst, stable=True)
        src = src[_o]
        dst = dst[_o]
        edge_attr_16 = jax.random.uniform(jax.random.fold_in(_gk, 11), (100000, 16), jnp.float32, 0.0, 1)
        return (x, src, dst, edge_attr_16)
    x, src, dst, edge_attr_16 = _rec_inputs()

    def _L0_gnn_setup():
        import jax, jax.numpy as jnp
        import numpy as np
        N_ATOMS = 50000
        N_PAIRS = 25000
        F = 64
        R = 16
        N_RES = 3

        def ssp(x):
            return jax.nn.softplus(x) - jnp.log(2.0).astype(x.dtype)
        key = jax.random.key(seed)
        ks = jax.random.split(key, 16)
        s = 0.1
        return {'atomic_embedding': jax.random.normal(ks[0], (N_ATOMS, F), jnp.float32), 'f_ij': jax.random.uniform(ks[1], (N_PAIRS, R), jnp.float32), 'pair_indices': jax.random.randint(ks[2], (2, N_PAIRS), 0, N_ATOMS, jnp.int32), 'W_att': jax.random.normal(ks[3], (F, R), jnp.float32) * s, 'W_i': jax.random.normal(ks[4], (F, F), jnp.float32) * s, 'b_i': jnp.zeros((F,), jnp.float32), 'W_j': jax.random.normal(ks[5], (F, F), jnp.float32) * s, 'b_j': jnp.zeros((F,), jnp.float32), 'W_v': jax.random.normal(ks[6], (F, F), jnp.float32) * s, 'b_v': jnp.zeros((F,), jnp.float32), 'res_dense_W': jax.random.normal(ks[7], (N_RES, F, F), jnp.float32) * s, 'res_dense_b': jnp.zeros((N_RES, F), jnp.float32), 'res_res_W': jax.random.normal(ks[8], (N_RES, F, F), jnp.float32) * s, 'res_res_b': jnp.zeros((N_RES, F), jnp.float32), 'gate': jnp.ones((F,), jnp.float32)}
    _L0_gnn_all = _L0_gnn_setup()
    _L0_gnn_in = {k: v for k, v in _L0_gnn_all.items() if k in ('W_att', 'W_i', 'b_i', 'W_j', 'b_j', 'W_v', 'b_v', 'res_dense_W', 'res_dense_b', 'res_res_W', 'res_res_b', 'gate')}
    del _L0_gnn_all

    def _L1_gnn_setup():
        import jax, jax.numpy as jnp
        import numpy as np
        N, E, D, H, C = (50000, 25000, 64, 2, 64)

        def _transformer_conv(x, src, dst, wq, bq, wk, bk, wv, bv, ws, bs):
            n = x.shape[0]
            q = (x @ wq + bq).reshape(n, H, C)
            k = (x @ wk + bk).reshape(n, H, C)
            v = (x @ wv + bv).reshape(n, H, C)
            qi = q[dst]
            kj = k[src]
            vj = v[src]
            alpha = jnp.einsum('ehc,ehc->eh', qi, kj) / jnp.sqrt(jnp.asarray(C, x.dtype))
            amax = jax.ops.segment_max(alpha, dst, num_segments=n)
            amax = jnp.where(jnp.isfinite(amax), amax, 0.0)
            ex = jnp.exp(alpha - amax[dst])
            denom = jax.ops.segment_sum(ex, dst, num_segments=n)
            a = ex / (denom[dst] + 1e-16)
            out = jax.ops.segment_sum(a[:, :, None] * vj, dst, num_segments=n)
            out = out.mean(axis=1)
            return out + x @ ws + bs
        key = jax.random.key(seed)
        ks = jax.random.split(key, 20)
        x = jax.random.normal(ks[0], (N, D), dtype=jnp.float32)
        edge_index = jax.random.randint(ks[1], (2, E), 0, N, dtype=jnp.int64)
        s = 1.0 / np.sqrt(D)

        def lin(k, din, dout):
            return jax.random.uniform(k, (din, dout), jnp.float32, -s, s)
        inp = {'x': x, 'edge_index': edge_index}
        i = 2
        for l, din in ((1, D), (2, C)):
            for nm, dout in (('wq', H * C), ('wk', H * C), ('wv', H * C), ('ws', C)):
                inp[f'l{l}_{nm}'] = lin(ks[i], din, dout)
                i += 1
                inp[f"l{l}_{nm.replace('w', 'b')}"] = jnp.zeros((dout,), jnp.float32)
        return inp
    _L1_gnn_all = _L1_gnn_setup()
    _L1_gnn_in = {k: v for k, v in _L1_gnn_all.items() if k in ('l1_wq', 'l1_bq', 'l1_wk', 'l1_bk', 'l1_wv', 'l1_bv', 'l1_ws', 'l1_bs', 'l2_wq', 'l2_bq', 'l2_wk', 'l2_bk', 'l2_wv', 'l2_bv', 'l2_ws', 'l2_bs')}
    del _L1_gnn_all
    return {'x': x, 'src': src, 'dst': dst, 'edge_attr_16': edge_attr_16, 'L0_gnn_W_att': _L0_gnn_in['W_att'], 'L0_gnn_W_i': _L0_gnn_in['W_i'], 'L0_gnn_b_i': _L0_gnn_in['b_i'], 'L0_gnn_W_j': _L0_gnn_in['W_j'], 'L0_gnn_b_j': _L0_gnn_in['b_j'], 'L0_gnn_W_v': _L0_gnn_in['W_v'], 'L0_gnn_b_v': _L0_gnn_in['b_v'], 'L0_gnn_res_dense_W': _L0_gnn_in['res_dense_W'], 'L0_gnn_res_dense_b': _L0_gnn_in['res_dense_b'], 'L0_gnn_res_res_W': _L0_gnn_in['res_res_W'], 'L0_gnn_res_res_b': _L0_gnn_in['res_res_b'], 'L0_gnn_gate': _L0_gnn_in['gate'], 'L1_gnn_l1_wq': _L1_gnn_in['l1_wq'], 'L1_gnn_l1_bq': _L1_gnn_in['l1_bq'], 'L1_gnn_l1_wk': _L1_gnn_in['l1_wk'], 'L1_gnn_l1_bk': _L1_gnn_in['l1_bk'], 'L1_gnn_l1_wv': _L1_gnn_in['l1_wv'], 'L1_gnn_l1_bv': _L1_gnn_in['l1_bv'], 'L1_gnn_l1_ws': _L1_gnn_in['l1_ws'], 'L1_gnn_l1_bs': _L1_gnn_in['l1_bs'], 'L1_gnn_l2_wq': _L1_gnn_in['l2_wq'], 'L1_gnn_l2_bq': _L1_gnn_in['l2_bq'], 'L1_gnn_l2_wk': _L1_gnn_in['l2_wk'], 'L1_gnn_l2_bk': _L1_gnn_in['l2_bk'], 'L1_gnn_l2_wv': _L1_gnn_in['l2_wv'], 'L1_gnn_l2_bv': _L1_gnn_in['l2_bv'], 'L1_gnn_l2_ws': _L1_gnn_in['l2_ws'], 'L1_gnn_l2_bs': _L1_gnn_in['l2_bs']}

def reference(x, src, dst, edge_attr_16, L0_gnn_W_att, L0_gnn_W_i, L0_gnn_b_i, L0_gnn_W_j, L0_gnn_b_j, L0_gnn_W_v, L0_gnn_b_v, L0_gnn_res_dense_W, L0_gnn_res_dense_b, L0_gnn_res_res_W, L0_gnn_res_res_b, L0_gnn_gate, L1_gnn_l1_wq, L1_gnn_l1_bq, L1_gnn_l1_wk, L1_gnn_l1_bk, L1_gnn_l1_wv, L1_gnn_l1_bv, L1_gnn_l1_ws, L1_gnn_l1_bs, L1_gnn_l2_wq, L1_gnn_l2_bq, L1_gnn_l2_wk, L1_gnn_l2_bk, L1_gnn_l2_wv, L1_gnn_l2_bv, L1_gnn_l2_ws, L1_gnn_l2_bs):
    import jax
    import jax.numpy as jnp

    def _L0_gnn_ref(atomic_embedding, f_ij, pair_indices, W_att, W_i, b_i, W_j, b_j, W_v, b_v, res_dense_W, res_dense_b, res_res_W, res_res_b, gate):
        import jax, jax.numpy as jnp
        import numpy as np
        N_ATOMS = 50000
        N_PAIRS = 25000
        F = 64
        R = 16
        N_RES = 3

        def ssp(x):
            return jax.nn.softplus(x) - jnp.log(2.0).astype(x.dtype)
        x = atomic_embedding
        idx_i = pair_indices[0]
        idx_j = pair_indices[1]
        n_atoms = x.shape[0]
        xa = ssp(x)
        g = jnp.einsum('pr,fr->pf', f_ij, W_att)
        x_i = ssp(jnp.einsum('nf,gf->ng', xa, W_i) + b_i)
        x_j = ssp(jnp.einsum('nf,gf->ng', xa, W_j) + b_j)
        msg = x_j[idx_j] * g
        m = x_i + jax.ops.segment_sum(msg, idx_i, num_segments=n_atoms)
        for k in range(res_dense_W.shape[0]):
            h = ssp(jnp.einsum('nf,gf->ng', m, res_dense_W[k]) + res_dense_b[k])
            m = m + jnp.einsum('nf,gf->ng', h, res_res_W[k]) + res_res_b[k]
        m = ssp(m)
        return gate * x + jnp.einsum('nf,gf->ng', m, W_v) + b_v

    def _L1_gnn_ref(x, edge_index, l1_wq, l1_bq, l1_wk, l1_bk, l1_wv, l1_bv, l1_ws, l1_bs, l2_wq, l2_bq, l2_wk, l2_bk, l2_wv, l2_bv, l2_ws, l2_bs):
        import jax, jax.numpy as jnp
        import numpy as np
        N, E, D, H, C = (50000, 25000, 64, 2, 64)

        def _transformer_conv(x, src, dst, wq, bq, wk, bk, wv, bv, ws, bs):
            n = x.shape[0]
            q = (x @ wq + bq).reshape(n, H, C)
            k = (x @ wk + bk).reshape(n, H, C)
            v = (x @ wv + bv).reshape(n, H, C)
            qi = q[dst]
            kj = k[src]
            vj = v[src]
            alpha = jnp.einsum('ehc,ehc->eh', qi, kj) / jnp.sqrt(jnp.asarray(C, x.dtype))
            amax = jax.ops.segment_max(alpha, dst, num_segments=n)
            amax = jnp.where(jnp.isfinite(amax), amax, 0.0)
            ex = jnp.exp(alpha - amax[dst])
            denom = jax.ops.segment_sum(ex, dst, num_segments=n)
            a = ex / (denom[dst] + 1e-16)
            out = jax.ops.segment_sum(a[:, :, None] * vj, dst, num_segments=n)
            out = out.mean(axis=1)
            return out + x @ ws + bs
        src, dst = (edge_index[0], edge_index[1])
        h = _transformer_conv(x, src, dst, l1_wq, l1_bq, l1_wk, l1_bk, l1_wv, l1_bv, l1_ws, l1_bs)
        h = _transformer_conv(h, src, dst, l2_wq, l2_bq, l2_wk, l2_bk, l2_wv, l2_bv, l2_ws, l2_bs)
        return h
    edge_index = jnp.stack([src, dst])
    x = _layernorm(x + _L0_gnn_ref(x, edge_attr_16, edge_index, L0_gnn_W_att, L0_gnn_W_i, L0_gnn_b_i, L0_gnn_W_j, L0_gnn_b_j, L0_gnn_W_v, L0_gnn_b_v, L0_gnn_res_dense_W, L0_gnn_res_dense_b, L0_gnn_res_res_W, L0_gnn_res_res_b, L0_gnn_gate), axis=-1)
    x = _layernorm(x + _L1_gnn_ref(x, edge_index, L1_gnn_l1_wq, L1_gnn_l1_bq, L1_gnn_l1_wk, L1_gnn_l1_bk, L1_gnn_l1_wv, L1_gnn_l1_bv, L1_gnn_l1_ws, L1_gnn_l1_bs, L1_gnn_l2_wq, L1_gnn_l2_bq, L1_gnn_l2_wk, L1_gnn_l2_bk, L1_gnn_l2_wv, L1_gnn_l2_bv, L1_gnn_l2_ws, L1_gnn_l2_bs), axis=-1)
    return x

_drawn_inputs = setup_inputs


def setup_inputs(seed=0):
    import zlib

    import numpy as np

    out = dict(_drawn_inputs(seed))
    spreads = {'L0_gnn_b_i': (0.0, 0.545),
     'L0_gnn_b_j': (0.0, 0.1),
     'L0_gnn_b_v': (0.0, 0.1),
     'L0_gnn_res_dense_b': (0.0, 0.455),
     'L0_gnn_res_res_b': (0.0, 0.1),
     'L0_gnn_gate': (1.0, 0.2),
     'L1_gnn_l1_bq': (0.0, 0.8),
     'L1_gnn_l1_bk': (0.0, 0.8),
     'L1_gnn_l1_bv': (0.0, 0.1),
     'L1_gnn_l1_bs': (0.0, 0.1),
     'L1_gnn_l2_bq': (0.0, 0.8),
     'L1_gnn_l2_bk': (0.0, 0.8),
     'L1_gnn_l2_bv': (0.0, 0.1),
     'L1_gnn_l2_bs': (0.0, 0.1)}
    factors = {'L1_gnn_l1_wq': 3.473, 'L1_gnn_l1_wk': 3.438, 'L1_gnn_l2_wq': 8.0, 'L1_gnn_l2_wk': 8.0}
    for name, (base, spread) in spreads.items():
        noise = np.random.default_rng([zlib.crc32(name.encode()), seed]).standard_normal(out[name].shape)
        drawn = base * np.exp(spread * noise) if base else spread * noise
        out[name] = jnp.asarray(drawn.astype(out[name].dtype))
    for name, factor in factors.items():
        out[name] = (out[name] * factor).astype(out[name].dtype)
    return out
```

```python
from contextlib import ExitStack

import concourse.bass as bass
from concourse import mybir

N = 3125
E = 100000
F = 64
R = 16
P = 125
NT = N // P
EJ = E // P
G = 8
NG = EJ // G
HALF = (NT + 1) // 2
HC = HALF * P
LC = HC // 5
D = 450
NC = -(-N // D)
ND = NC * D
DP = D // NT
DB = D // 5
RING = 5
ACCS = G
BIG = 1e30
FLOOR = -1e20
HEADS = 2
EXP_LN_SET = 6
VW = F + 1
ATT = NC * NT


def build(nc, x, src, dst, edge_attr, W_att, W_i, b_i, W_j, b_j, W_v, b_v, rd_W, rd_b, rr_W, rr_b, gate,
          wq1, bq1, wk1, bk1, wv1, bv1, ws1, bs1, wq2, bq2, wk2, bk2, wv2, bv2, ws2, bs2, out):
    f32 = mybir.dt.float32
    f16 = mybir.dt.float16
    i32 = mybir.dt.int32
    ALU = mybir.AluOpType
    ACT = mybir.ActivationFunctionType
    AX = mybir.AxisListType.X
    layers = [(wq1, bq1, wk1, bk1, wv1, bv1, ws1, bs1), (wq2, bq2, wk2, bk2, wv2, bv2, ws2, bs2)]

    xj_dram = nc.dram_tensor("xj_rows", [N, F], f32, kind="Internal").ap()
    acc_dram = [nc.dram_tensor(f"message_sums{u}", [N + P, F], f32, kind="Internal").ap() for u in range(ACCS)]
    cnt_dram = nc.dram_tensor("edge_counts", [N * ND + P, 1], f32, kind="Internal").ap()
    cnt_rows = cnt_dram[0:N * ND, :].rearrange("(p t d) o -> p t (d o)", p=P, t=NT)

    ctx = ExitStack()
    with ctx:
        ctx.enter_context(nc.allow_non_contiguous_dma(reason="short bias columns"))

        def sb(name, cols, dt=f32):
            return ctx.enter_context(nc.sbuf_tensor(name, [128, cols], dt))

        sems = {}

        def sem(name):
            if name not in sems:
                sems[name] = ctx.enter_context(nc.semaphore(name))
            return sems[name]

        T = sb("scores", NT * HEADS * D)
        Xt = sb("x_nodes", (NT + 1) * F)
        X1t = sb("x1_nodes", NT * F)
        Ht = sb("h_nodes", NT * F)
        SKt = sb("skip_nodes", NT * F)
        hTt = sb("h_features", ND)
        qTt = sb("q_features", ND)
        kTt = sb("k_features", ND)
        Vt = sb("v_nodes", NT * HEADS * VW)
        O1t = sb("attended1", ND)
        Rt = sb("running_max", HEADS * D)
        MBt = sb("max_of_targets", HEADS * D)
        CL = sb("counts_and_logs", 2 * RING * D)
        qct = sb("q_chunk", D)
        WL = sb("layer_weights", 2 * (128 + 128 + 192))
        BC = sb("bias_columns", 12)
        ident = sb("identity", 128)
        identh = sb("identity16", 128, f16)
        small = sb("small", 192)
        halfc = sb("half_column", 1)
        kh = sb("keys16", 2 * G, f16)
        PS = ctx.enter_context(nc.psum_tensor("PS", [128, 8, 512], f32))

        def grid(t, a, off=0, b=None, parts=128):
            return t[0:parts, off:off + a * b].rearrange("p (a b) -> p a b", b=b)

        X = Xt[0:P, :].rearrange("p (j h f) -> p j h f", h=2, f=F)
        X1 = grid(X1t, NT, 0, F, P)
        H = grid(Ht, NT, 0, F, P)
        SK = grid(SKt, NT, 0, F, P)
        BD = grid(SKt, 9, 0, 128)
        BDraw = grid(T, 9, 0, 128)
        xT2 = O1t[:, 0:HC]
        M = kTt[:, 0:HC]
        Z = qTt[:, 0:HC]
        LG = Vt[:, 0:HC]
        XA = hTt[:, 0:HC]
        XJ = T[:, 1200:1200 + HC]
        XJn = grid(T, NT + 1, 3000, F, P)
        zero_tile = T[0:P, 5000:5000 + 26 * F]
        cfill = CL[0:P, 0:ND]

        at = [7000]

        def take(n):
            at[0] += n
            return at[0] - n

        o = take(EJ)
        src_i = T[0:P, o:o + EJ].bitcast(i32)
        o = take(EJ)
        dst_i = T[0:P, o:o + EJ].bitcast(i32)
        SelS = grid(T, G, take(G * P), P, P)
        SelD = grid(T, G, take(G * P), P, P)
        SelP = grid(T, G, take(G * P), P, P)
        tmpP = grid(T, G, take(G * P), P, P)
        tmpS = grid(T, G, take(G * P), P, P)
        gx = [T[0:P, o:o + G * F] for o in (take(G * F), take(G * F))]
        msg = grid(T, G, take(G * F), F, P)
        cm = [T[0:P, o:o + G * F] for o in (take(G * F), take(G * F))]
        f8 = [T[0:P, o:o + G * R] for o in (take(G * R), take(G * R))]
        o = take(P)
        fT = T[:, o:o + P]
        o = take(G * F)
        Wblk = T[:, o:o + G * F]
        o = take(P)
        low = T[0:P, o:o + P]
        o = take(R)
        Watt = T[0:F, o:o + R]
        o = take(F)
        WattT = T[0:R, o:o + F]
        assert at[0] <= NT * HEADS * D
        sc = [0]

        def col(n, parts=P):
            sc[0] += n
            assert sc[0] <= 192
            return small[0:parts, sc[0] - n:sc[0]]

        srcf, dstf, tS, tC, base, sumC, preS, preP = (col(G) for _ in range(8))
        dcur = [col(G).bitcast(i32) for _ in range(2)]
        sidx = [col(G).bitcast(i32) for _ in range(2)]
        cidx = [col(G).bitcast(i32) for _ in range(2)]
        cnt = [col(G) for _ in range(2)]
        trash_i = col(2).bitcast(i32)
        trash = col(2)
        srch, dsth = kh[0:P, 0:G], kh[0:P, G:2 * G]

        ACC = [grid(T, NT, u * NT * F, F, P) for u in range(ACCS)]
        AGG = X

        Tt = T[0:P, :].rearrange("p (i h d) -> p i h d", i=NT, h=HEADS)
        RM = Rt[0:P, :].rearrange("p (h d) -> p h d", h=HEADS)
        MB = MBt[0:P, :].rearrange("p (h d) -> p h d", h=HEADS)
        Cb = [CL[0:P, r * D:(r + 1) * D] for r in range(RING)]
        Lb = [CL[0:P, (RING + r) * D:(RING + r + 1) * D] for r in range(RING)]
        hT = hTt[0:F + 1, :]
        qT, kT, qc = qTt[:, :], kTt[:, :].rearrange("c (t p) -> c t p", t=NT), qct[:, :]
        V = Vt[0:P, :].rearrange("p (t h c) -> p t h c", t=NT, h=HEADS)
        OT = [hTt[0:VW, :], O1t[0:VW, :]]
        mrow = small[0:DB, 160:170]
        NDn = T[0:P, 0:NT * HEADS * VW].rearrange("p (t h c) -> p t h c", t=NT, h=HEADS)
        rec = T[0:P, 4000:4000 + NT * HEADS].rearrange("p (t h) -> p t h", t=NT)
        att = grid(T, NT * HEADS, 5000, F, P)
        att4 = T[0:P, 5000:5000 + NT * HEADS * F].rearrange("p (t h c) -> p t h c", t=NT, h=HEADS)
        lnsum, lnvar = T[0:P, 9000:9000 + NT], T[0:P, 9100:9100 + NT]
        lnsq = grid(T, NT, 10000, F, P)

        def wq_(l):
            return WL[0:F + 1, l * 448:l * 448 + 128]

        def wk_(l):
            return WL[0:F + 1, l * 448 + 128:l * 448 + 256]

        def wv_(l):
            return WL[0:F + 1, l * 448 + 256:l * 448 + 448]

        pairs = [PS[:, 0:3, 0:500], PS[:, 3:4, 0:P]]
        block_at = [PS[:, j // 4, (j % 4) * P:(j % 4 + 1) * P] for j in range(HALF)]
        node_at = [PS[0:P, j // 4, (j % 4) * 128:(j % 4 + 1) * 128] for j in range(HALF)]
        lin5 = PS[:, 0:5, 0:LC]

        def five(v):
            return v.rearrange("p (a b) -> p a b", a=5)

        block = ctx.enter_context(nc.Block())

        @block.sync
        def _(sp):
            xv = x.rearrange("(p t) f -> p t f", p=P)
            sp.dma_start(X[:, :, 0, :], xv[:, 0:HALF, :]).then_inc(sem("x_loaded"), 16)
            sp.dma_start(X[:, 0:NT - HALF, 1, :], xv[:, HALF:NT, :]).then_inc(sem("x_loaded"), 16)
            sp.wait_ge(sem("bd_zeroed"), 1)
            for h in range(2):
                q = slice(64 * h, 64 * h + 64)
                for i, w in enumerate((W_i, W_j, W_v)):
                    sp.dma_start(BDraw[q, i, q], w).then_inc(sem("weights_loaded"), 16)
                for i, w in ((3, rd_W), (6, rr_W)):
                    sp.dma_start(BDraw[q, i:i + 3, q], w.rearrange("k g f -> g k f")).then_inc(sem("weights_loaded"), 16)
                for i, b in enumerate((b_i, b_j, b_v, gate)):
                    sp.dma_start(BC[q, i:i + 1], b.rearrange("(f o) -> f o", o=1)).then_inc(sem("weights_loaded"), 16)
                for i, b in ((4, rd_b), (7, rr_b)):
                    sp.dma_start(BC[q, i:i + 3], b.rearrange("k f -> f k")).then_inc(sem("weights_loaded"), 16)
            sp.dma_start(Watt, W_att).then_inc(sem("watt_loaded"), 16)
            sp.dma_start(src_i, src.rearrange("(p j) -> p j", p=P)).then_inc(sem("edges_loaded"), 16)
            sp.dma_start(dst_i, dst.rearrange("(p j) -> p j", p=P)).then_inc(sem("edges_loaded"), 16)
            for l, (wq, bq, wk, bk, wv, bv, ws, bs) in enumerate(layers):
                for w, b, dest in ((wq, bq, wq_(l)), (wk, bk, wk_(l)), (wv, bv, wv_(l)[:, 0:128]), (ws, bs, wv_(l)[:, 128:192])):
                    sp.dma_start(dest[0:F, :], w).then_inc(sem("layer_weights"), 16)
                    sp.dma_start(dest[F:F + 1, :], b.rearrange("(o f) -> o f", o=1)).then_inc(sem("layer_weights"), 16)
            sp.wait_ge(sem("fills_set"), 2)
            for u in range(ACCS):
                sp.dma_start(acc_dram[u].rearrange("(p t) f -> p (t f)", p=P), zero_tile).then_inc(sem("sums_cleared"), 16)
            for t in range(NT):
                sp.dma_start(cnt_rows[:, t, :], cfill).then_inc(sem("counts_cleared"), 16)
            sp.dma_start(cnt_dram[N * ND:N * ND + P, :], cfill[:, 0:1]).then_inc(sem("counts_cleared"), 16)
            sp.wait_ge(sem("xj_nodes"), 1)
            sp.dma_start(xj_dram.rearrange("(p t) f -> p t f", p=P), XJn[:, 0:NT, :]).then_inc(sem("xj_stored"), 16)
            sp.wait_ge(sem("wblk_zeroed"), 1)
            sp.wait_ge(sem("wattT_copied"), 1)
            for j in range(G):
                sp.dma_start(Wblk[R * j:R * j + R, F * j:F * j + F], WattT).then_inc(sem("wblk_ready"), 16)

            fe = edge_attr.rearrange("(p j) r -> p (j r)", p=P)

            def load_f(g, u, first):
                if not first:
                    sp.wait_ge(sem("fT_in_psum"), g - 1)
                sp.dma_start(f8[u], fe[:, bass.ds(g * (G * R), G * R)]).then_inc(sem(f"f_loaded{u}"), 16)

            for u in range(2):
                load_f(u, u, True)
            with sp.Fori(1, NG // 2) as k:
                for u in range(2):
                    load_f(2 * k + u, u, False)

            for u in range(ACCS):
                sp.wait_ge(sem(f"sum_added{u}"), 16 * NG)
                sp.dma_start(ACC[u], acc_dram[u][0:N, :].rearrange("(p t) f -> p t f", p=P)).then_inc(sem(f"sums_loaded{u}"), 16)

            sp.wait_ge(sem("count_added"), 16 * EJ)
            for l in range(2):
                def load_c(c, i, first):
                    n = l * ATT + c * NT + i
                    r = i % RING
                    if not first:
                        sp.wait_ge(sem("log_ready"), n - RING + 1)
                    sp.dma_start(Cb[r], cnt_rows[:, i, bass.ds(c * D, D)]).then_inc(sem(f"count_loaded{r}"), 16)

                for i in range(NT):
                    load_c(0, i, l == 0 and i < RING)
                with sp.Fori(1, NC) as c:
                    for i in range(NT):
                        load_c(c, i, False)
            sp.wait_ge(sem("result_ready"), 1)
            sp.dma_start(out.rearrange("(p t) f -> p t f", p=P), H).then_inc(sem("stored"), 16)
            sp.wait_ge(sem("stored"), 16)

        @block.gpsimd
        def _(pool):
            nc.gpsimd.memset(BDraw, 0.0).then_inc(sem("bd_zeroed"), 1)
            nc.gpsimd.memset(ident[:, :], 0.0).then_inc(sem("ident_zeroed"), 1)
            pool.wait_ge(sem("ident_zeroed"), 1)
            nc.gpsimd.affine_select(out=ident[:, :], in_=ident[:, :], compare_op=ALU.not_equal, fill=1.0, base=0,
                                    pattern=[[-1, 128]], channel_multiplier=1).then_inc(sem("ident_ready"), 1)
            nc.gpsimd.memset(zero_tile, 0.0).then_inc(sem("fills_set"), 1)
            nc.gpsimd.memset(cfill, -0.5).then_inc(sem("fills_set"), 1)
            nc.gpsimd.memset(Wblk, 0.0).then_inc(sem("wblk_zeroed"), 1)
            nc.gpsimd.memset(low, 1.0).then_inc(sem("low_set"), 1)
            pool.wait_ge(sem("low_set"), 1)
            nc.gpsimd.affine_select(out=low, in_=low, compare_op=ALU.is_gt, fill=0.0, base=0,
                                    pattern=[[-1, P]], channel_multiplier=1).then_inc(sem("low_ready"), 1)
            nc.gpsimd.iota(trash_i[:, 0:1], pattern=[[0, 1]], base=N, channel_multiplier=1).then_inc(sem("trash_iota"), 1)
            nc.gpsimd.iota(trash_i[:, 1:2], pattern=[[0, 1]], base=N * ND, channel_multiplier=1).then_inc(sem("trash_iota"), 1)

            def settled():
                pool.sem_inc(sem("pool_waited"), 1)

            def gather(g, u, s):
                pool.indirect_dma_start(gx[u][:, s * F:(s + 1) * F], None, xj_dram,
                                        bass.IndirectOffsetOnAxis(ap=dcur[u][:, s:s + 1], axis=0)
                                        ).then_inc(sem(f"gathered{u}"), 16)

            def scatter(g, u, s):
                pool.wait_ge(sem(f"sum_added{s}"), 16 * g)
                settled()
                pool.indirect_dma_start(acc_dram[s], bass.IndirectOffsetOnAxis(ap=sidx[u][:, s:s + 1], axis=0),
                                        cm[u][:, s * F:(s + 1) * F], None, compute_op=ALU.add
                                        ).then_inc(sem(f"sum_added{s}"), 16)
                pool.wait_ge(sem("count_added"), 16 * G * g + 16 * s)
                settled()
                pool.indirect_dma_start(cnt_dram, bass.IndirectOffsetOnAxis(ap=cidx[u][:, s:s + 1], axis=0),
                                        cnt[u][:, s:s + 1], None, compute_op=ALU.add
                                        ).then_inc(sem("count_added"), 16)

            def group(g, u, gathers, scatters):
                if gathers:
                    pool.wait_ge(sem("staged"), g + 1)
                if scatters:
                    pool.wait_ge(sem("combined"), g - 1)
                    pool.wait_ge(sem("indexed"), g - 1)
                settled()
                for s in range(G):
                    if gathers:
                        gather(g, u, s)
                    if scatters:
                        scatter(g - 2, u, s)

            pool.wait_ge(sem("xj_stored"), 16)
            for u in range(2):
                group(u, u, True, False)
            pool.wait_ge(sem("sums_cleared"), 16 * ACCS)
            pool.wait_ge(sem("counts_cleared"), 16 * (NT + 1))
            for u in range(2):
                group(2 + u, u, True, True)
            with pool.Fori(2, NG // 2) as k:
                for u in range(2):
                    group(2 * k + u, u, True, True)
            for u in range(2):
                group(NG + u, u, False, True)

            for l in range(2):
                def shift(c, i):
                    if i == 0:
                        pool.wait_ge(sem("max_spread"), l * NC + c + 1)
                    nc.gpsimd.tensor_tensor(Tt[:, i], Tt[:, i], MB, ALU.subtract).then_inc(sem("shifted"), 1)

                with pool.Fori(1, NC) as c:
                    for i in range(NT):
                        shift(c - 1, i)
                for i in range(NT):
                    shift(NC - 1, i)

        @block.scalar
        def _(act):
            ssp_n, lin_n = [0], [0]

            def load_exp_ln():
                act.add_instruction(mybir.InstLoadActFuncSet(name=nc.get_next_instruction_name(), engine=mybir.EngineType.Activation, act_func_set_id=EXP_LN_SET, ins=[], outs=[]))

            load_exp_ln()

            def ssp(z):
                k = ssp_n[0]
                ssp_n[0] += 1
                act.wait_ge(sem("ssp_done"), k)
                nc.scalar.activation(LG, z, ACT.Abs).then_inc(sem("ssp_abs"), 1)
                act.wait_ge(sem("ssp_abs"), k + 1)
                nc.scalar.activation(LG, LG, ACT.Exp, scale=-1.0).then_inc(sem("ssp_exp"), 1)
                act.wait_ge(sem("ssp_exp"), k + 1)
                nc.scalar.activation(LG, LG, ACT.Ln, scale=0.5, bias=halfc[:, :]).then_inc(sem("ssp_ln"), 1)

            def lin_bias(b):
                lin_n[0] += 1
                act.wait_ge(sem("lin_done"), lin_n[0])
                act.wait_ge(sem("ssp_done"), ssp_n[0])
                nc.scalar.activation(five(Z), lin5, ACT.Identity, bias=BC[:, b:b + 1]).then_inc(sem("lin_used"), 1)
                act.wait_ge(sem("lin_used"), lin_n[0])

            act.wait_ge(sem("x_blocks"), 1)
            nc.scalar.activation(xT2[:, 0:1500].rearrange("p (a b) -> p a b", a=3), pairs[0], ACT.Copy).then_inc(sem("xT_copied"), 1)
            nc.scalar.activation(xT2[:, 1500:HC].rearrange("p (a b) -> p a b", a=1), pairs[1], ACT.Copy).then_inc(sem("xT_copied"), 1)
            act.wait_ge(sem("xT_copied"), 2)
            act.wait_ge(sem("half_set"), 1)
            ssp(xT2)
            act.wait_ge(sem("bd_in_psum"), 1)
            nc.scalar.activation(BD[:, 0:8, :].rearrange("p (a b) c -> p a (b c)", a=2), PS[:, 4:6, :], ACT.Copy).then_inc(sem("bd_ready"), 1)
            nc.scalar.activation(BD[:, 8, :], PS[:, 6, 0:128], ACT.Copy).then_inc(sem("bd_ready"), 1)
            act.wait_ge(sem("watt_in_psum"), 1)
            nc.scalar.activation(WattT, PS[0:R, 7, 0:F], ACT.Copy).then_inc(sem("wattT_copied"), 1)
            lin_bias(1)
            ssp(Z)
            act.wait_ge(sem("xj_in_psum"), 1)
            for h in range(2):
                nc.scalar.activation(XJn[:, HALF * h:HALF * h + 12, :].rearrange("p (a b) f -> p a b f", a=3),
                                     PS[0:P, 0:3, :].rearrange("p a (b h f) -> p a b h f", h=2, f=F)[:, :, :, h, :],
                                     ACT.Copy).then_inc(sem("xj_part"), 1)
                nc.scalar.activation(XJn[:, HALF * h + 12, :], PS[0:P, 3, F * h:F * h + F], ACT.Copy).then_inc(sem("xj_part"), 1)
            act.wait_ge(sem("xj_part"), 4)
            act.sem_inc(sem("xj_nodes"), 1)
            lin_bias(0)
            ssp(Z)

            def edge_group(g, u, first):
                act.wait_ge(sem("fT_in_psum"), g + 1)
                act.wait_ge(sem("g_in_psum"), g)
                nc.scalar.activation(fT, PS[:, 4, 0:P], ACT.Copy).then_inc(sem("fT_copied"), 1)
                act.wait_ge(sem("comb_in_psum"), g + 1)
                if not first:
                    for s in range(ACCS):
                        act.wait_ge(sem(f"sum_added{s}"), 16 * (g - 1))
                nc.scalar.activation(cm[u], PS[0:P, 6, :], ACT.Copy).then_inc(sem("combined"), 1)

            for u in range(2):
                edge_group(u, u, True)
            with act.Fori(1, NG // 2) as k:
                for u in range(2):
                    edge_group(2 * k + u, u, False)

            for k in range(3):
                lin_bias(4 + k)
                ssp(Z)
                lin_n[0] += 1
            act.wait_ge(sem("m_updated"), 4)
            ssp(M)
            lin_bias(2)
            act.wait_ge(sem("y_in_psum"), 1)
            for h in range(2):
                nc.scalar.activation(H[:, HALF * h:HALF * h + 12, :].rearrange("p (a b) f -> p a b f", a=3),
                                     PS[0:P, 0:3, :].rearrange("p a (b h f) -> p a b h f", h=2, f=F)[:, :, :, h, :],
                                     ACT.Copy).then_inc(sem("y_nodes"), 1)
            nc.scalar.activation(H[:, 12, :], PS[0:P, 3, 0:F], ACT.Copy).then_inc(sem("y_nodes"), 1)

            def ln_act(k):
                act.wait_ge(sem("ln_centered"), k + 1)
                nc.scalar.activation(lnsq, H, ACT.Square).then_inc(sem("ln_squared"), 1)
                act.wait_ge(sem("ln_var"), k + 1)
                nc.scalar.activation(lnvar, lnvar, ACT.Sqrt).then_inc(sem("ln_std"), 1)

            ln_act(0)
            load_exp_ln()

            for l in range(2):
                hv = hT[0:F, 0:N].rearrange("c (p t) -> c t p", t=NT)
                act.wait_ge(sem("hT_cleared"), l + 1)
                for b in range(7):
                    n = min(4, NT - 4 * b)
                    act.wait_ge(sem("h_block"), 7 * l + b + 1)
                    nc.scalar.activation(hv[:, 4 * b:4 * b + n, :],
                                         PS[0:F, b, 0:n * P].rearrange("c (t p) -> c t p", t=n), ACT.Copy
                                         ).then_inc(sem("hT_copied"), 1)
                for c in range(NC):
                    act.wait_ge(sem("qk_in_psum"), 2 * NC * l + 2 * c + 1)
                    nc.scalar.activation(qT[:, c * D:(c + 1) * D], PS[:, 0, 0:D], ACT.Copy, scale=0.125).then_inc(sem("qk_copied"), 1)
                    act.wait_ge(sem("qk_in_psum"), 2 * NC * l + 2 * c + 2)
                    nc.scalar.activation(kT[:, :, c * DP:(c + 1) * DP], PS[:, 1, 0:D].rearrange("c (p t) -> c t p", t=NT), ACT.Copy
                                         ).then_inc(sem("qk_copied"), 1)

                def logs(c, i):
                    n = l * ATT + c * NT + i
                    act.wait_ge(sem(f"count_loaded{i % RING}"), 16 * (NT // RING) * c + 16 * (l * ATT // RING + i // RING + 1))
                    if not (isinstance(n, int) and n < RING):
                        act.wait_ge(sem("log_ready"), n - RING + 1)
                    nc.scalar.activation(Lb[i % RING], Cb[i % RING], ACT.Abs).then_inc(sem("magnitude"), 1)
                    act.wait_ge(sem("magnitude"), n + 1)
                    nc.scalar.activation(Lb[i % RING], Lb[i % RING], ACT.Ln, bias=halfc[0:P, :]).then_inc(sem("logged"), 1)

                def exps(c, i):
                    n = l * ATT + c * NT + i
                    act.wait_ge(sem("shifted"), n + 1)
                    nc.scalar.activation(Tt[:, i], Tt[:, i], ACT.Exp).then_inc(sem("weighed"), 1)

                def stage(c, first, last):
                    if not last:
                        act.wait_ge(sem("scores_in_psum"), l * ATT + c * NT)
                        if isinstance(c, int) and c == 0:
                            act.wait_ge(sem("qk_copied"), 2 * NC * (l + 1))
                        nc.scalar.activation(qc, qT[:, bass.ds(c * D, D)], ACT.Copy).then_inc(sem("qc_ready"), 1)
                    for i in range(NT):
                        if not last:
                            logs(c, i)
                        if not first:
                            exps(c - 1, i)
                    if not last:
                        act.wait_ge(sem("max_in_psum"), l * NC + c + 1)
                        act.wait_ge(sem("shifted"), l * ATT + c * NT)
                        nc.scalar.activation(MB, PS[0:P, 6:8, 0:D], ACT.Copy).then_inc(sem("max_spread"), 1)
                    if not first:
                        act.wait_ge(sem("weighted_sums"), l * ATT + c * NT)
                        for h in range(HEADS):
                            nc.scalar.activation(OT[h][:, bass.ds((c - 1) * D, D)], PS[0:VW, 4 + h, 0:D], ACT.Copy
                                                 ).then_inc(sem("attended"), 1)

                stage(0, True, False)
                with act.Fori(1, NC) as c:
                    stage(c, False, False)
                stage(NC, False, True)
                for b in range(9):
                    n = min(3, NT - 3 * b)
                    act.wait_ge(sem("att_block"), 9 * l + b + 1)
                    nc.scalar.activation(NDn[:, 3 * b:3 * b + n].rearrange("p t h c -> p (t h c)"), PS[0:P, b % 8, 0:n * HEADS * VW], ACT.Copy
                                         ).then_inc(sem("att_copied"), 1)
            ln_act(1)

        @block.vector
        def _(dve):
            ssp_n, lin_n = [0], [0]

            def ssp(z, dest):
                ssp_n[0] += 1
                dve.wait_ge(sem("ssp_ln"), ssp_n[0])
                nc.vector.scalar_tensor_tensor(dest, z, 0.0, LG, ALU.max, ALU.add).then_inc(sem("ssp_done"), 1)

            chain = [0]

            def link(ins):
                chain[0] += 1
                ins.then_inc(sem("vector_chain"), 1)
                dve.wait_ge(sem("vector_chain"), chain[0])

            nc.vector.memset(halfc[:, :], 0.5).then_inc(sem("half_set"), 1)
            nc.vector.memset(X[:, HALF - 1, 1, :], 0.0).then_inc(sem("pad_zeroed"), 1)
            dve.wait_ge(sem("ident_ready"), 1)
            nc.vector.tensor_copy(identh[:, :], ident[:, :]).then_inc(sem("ident16_ready"), 1)
            dve.wait_ge(sem("trash_iota"), 2)
            nc.vector.tensor_copy(trash, trash_i).then_inc(sem("trash_ready"), 1)
            dve.wait_ge(sem("trash_ready"), 1)
            dve.wait_ge(sem("edges_loaded"), 32)

            def stage(g, u):
                sl = bass.ds(g * G, G)
                nc.vector.tensor_copy(srcf, src_i[:, sl]).then_inc(sem("keys_copied"), 1)
                nc.vector.tensor_copy(dstf, dst_i[:, sl]).then_inc(sem("keys_copied"), 1)
                nc.vector.tensor_copy(dcur[u], dst_i[:, sl]).then_inc(sem("keys_copied"), 1)
                nc.vector.tensor_scalar(srch, src_i[:, sl], float(-(N // 2)), None, ALU.add).then_inc(sem("keys_copied"), 1)
                nc.vector.tensor_scalar(dsth, dst_i[:, sl], float(-(N // 2)), None, ALU.add).then_inc(sem("keys_copied"), 1)
                dve.wait_ge(sem("keys_copied"), 5 * g + 5)
                dve.sem_inc(sem("staged"), 1)

            def compute(g, u, k, first, last):
                dve.wait_ge(sem("keys_in_psum"), g + 1)
                dve.wait_ge(sem("comb_in_psum"), g)
                for b in range(2):
                    q = slice(4 * b, 4 * b + 4)
                    for key, sel, bank in ((srch, SelS, b), (dsth, SelD, 2 + b)):
                        nc.vector.tensor_tensor(sel[:, q, :], PS[0:P, bank, 0:4 * P].rearrange("p (a b) -> p a b", a=4),
                                                key[:, q].unsqueeze(2).to_broadcast([P, 4, P]), ALU.is_equal
                                                ).then_inc(sem("matched"), 1)
                dve.wait_ge(sem("matched"), 4 * g + 4)
                nc.vector.tensor_tensor(SelP, SelS, SelD, ALU.mult).then_inc(sem("pairs"), 1)
                lowb = low.unsqueeze(1).to_broadcast([P, G, P])
                nc.vector.tensor_tensor(tmpS, SelS, lowb, ALU.mult).then_inc(sem("before_s"), 1)
                dve.wait_ge(sem("pairs"), g + 1)
                nc.vector.tensor_tensor(tmpP, SelP, lowb, ALU.mult).then_inc(sem("before_p"), 1)
                if not first:
                    dve.wait_ge(sem("count_added"), 16 * G * (g - 1))
                    for s in range(ACCS):
                        dve.wait_ge(sem(f"sum_added{s}"), 16 * (g - 1))
                nc.vector.tensor_reduce(cnt[u], SelP, AX, ALU.add).then_inc(sem("counted"), 1)
                dve.wait_ge(sem("before_s"), g + 1)
                nc.vector.tensor_reduce(preS, tmpS, AX, ALU.add).then_inc(sem("earlier"), 1)
                dve.wait_ge(sem("before_p"), g + 1)
                nc.vector.tensor_reduce(preP, tmpP, AX, ALU.add).then_inc(sem("earlier"), 1)
                nc.vector.scalar_tensor_tensor(base, srcf, float(ND), dstf, ALU.mult, ALU.add).then_inc(sem("cells"), 1)
                nc.vector.tensor_scalar(tS, srcf, -1.0, trash[:, 0:1], ALU.mult, ALU.add).then_inc(sem("to_trash"), 1)
                dve.wait_ge(sem("cells"), g + 1)
                nc.vector.tensor_scalar(tC, base, -1.0, trash[:, 1:2], ALU.mult, ALU.add).then_inc(sem("to_trash"), 1)
                dve.wait_ge(sem("to_trash"), 2 * g + 2)
                dve.wait_ge(sem("earlier"), 2 * g + 2)
                nc.vector.scalar_tensor_tensor(tS, preS, 0.0, tS, ALU.is_gt, ALU.mult).then_inc(sem("moved"), 1)
                nc.vector.scalar_tensor_tensor(tC, preP, 0.0, tC, ALU.is_gt, ALU.mult).then_inc(sem("moved"), 1)
                dve.wait_ge(sem("moved"), 2 * g + 2)
                nc.vector.tensor_tensor(sidx[u], tS, srcf, ALU.add).then_inc(sem("index_parts"), 1)
                nc.vector.tensor_tensor(cidx[u], tC, base, ALU.add).then_inc(sem("index_parts"), 1)
                dve.wait_ge(sem("counted"), g + 1)
                dve.wait_ge(sem("index_parts"), 2 * g + 2)
                dve.sem_inc(sem("indexed"), 1)
                if not last:
                    stage(g + 1, 1 - u)
                dve.wait_ge(sem(f"gathered{u}"), 16 * G * (k + 1))
                dve.wait_ge(sem("g_in_psum"), g + 1)
                nc.vector.tensor_tensor(msg.rearrange("p a b -> p (a b)"), gx[u], PS[0:P, 5, :], ALU.mult).then_inc(sem("messages"), 1)

            stage(0, 0)
            ssp(xT2, XA)
            ssp(Z, XJ)
            ssp(Z, M)
            dve.wait_ge(sem("low_ready"), 1)
            for u in range(2):
                compute(u, u, 0, True, False)
            with dve.Fori(1, NG // 2 - 1) as k:
                for u in range(2):
                    compute(2 * k + u, u, k, False, False)
            for u in range(2):
                compute(NG - 2 + u, u, NG // 2 - 1, False, u == 1)

            nc.vector.memset(AGG[:, HALF - 1, 1, :], 0.0).then_inc(sem("pad_zeroed"), 1)
            dve.wait_ge(sem("sums_loaded0"), 16)
            for u in range(1, ACCS - 1):
                dve.wait_ge(sem(f"sums_loaded{u}"), 16)
                link(nc.vector.tensor_tensor(ACC[0], ACC[0], ACC[u], ALU.add))
            dve.wait_ge(sem(f"sums_loaded{ACCS - 1}"), 16)
            nc.vector.tensor_tensor(AGG[:, :, 0, :], ACC[0][:, 0:HALF, :], ACC[ACCS - 1][:, 0:HALF, :], ALU.add).then_inc(sem("pad_zeroed"), 1)
            nc.vector.tensor_tensor(AGG[:, 0:NT - HALF, 1, :], ACC[0][:, HALF:NT, :], ACC[ACCS - 1][:, HALF:NT, :], ALU.add).then_inc(sem("pad_zeroed"), 1)
            dve.wait_ge(sem("pad_zeroed"), 4)
            dve.sem_inc(sem("sums_ready"), 1)
            dve.wait_ge(sem("sum_blocks"), 1)
            nc.vector.tensor_tensor(M[:, 0:1500].rearrange("p (a b) -> p a b", a=3), M[:, 0:1500].rearrange("p (a b) -> p a b", a=3),
                                    pairs[0], ALU.add).then_inc(sem("m_part"), 1)
            nc.vector.tensor_tensor(M[:, 1500:HC], M[:, 1500:HC], PS[:, 3, 0:P], ALU.add).then_inc(sem("m_part"), 1)
            dve.wait_ge(sem("m_part"), 2)
            dve.sem_inc(sem("m_updated"), 1)
            lin_n[0] = 2
            for k in range(3):
                ssp(Z, XA)
                lin_n[0] += 2
                dve.wait_ge(sem("lin_done"), lin_n[0])
                nc.vector.scalar_tensor_tensor(five(M), lin5, BC[:, 7 + k:8 + k], five(M), ALU.add, ALU.add).then_inc(sem("res_added"), 1)
                dve.wait_ge(sem("res_added"), k + 1)
                dve.sem_inc(sem("lin_used"), 1)
                dve.sem_inc(sem("m_updated"), 1)
            ssp(M, XA)
            dve.wait_ge(sem("lin_used"), 9)
            link(nc.vector.scalar_tensor_tensor(Z, xT2, BC[:, 3:4], Z, ALU.mult, ALU.add))
            nc.vector.tensor_tensor(Z, Z, xT2, ALU.add).then_inc(sem("y_ready"), 1)

            def layernorm(k, dest):
                link(nc.vector.tensor_reduce(lnsum, H, AX, ALU.add))
                link(nc.vector.tensor_scalar(lnsum, lnsum, 1.0 / F, None, ALU.mult))
                nc.vector.tensor_tensor(H, H, lnsum.unsqueeze(2).to_broadcast([P, NT, F]), ALU.subtract).then_inc(sem("ln_centered"), 1)
                dve.wait_ge(sem("ln_squared"), k + 1)
                link(nc.vector.tensor_reduce(lnvar, lnsq, AX, ALU.add))
                nc.vector.tensor_scalar(lnvar, lnvar, 1.0 / F, 1e-5, ALU.mult, ALU.add).then_inc(sem("ln_var"), 1)
                dve.wait_ge(sem("ln_std"), k + 1)
                link(nc.vector.reciprocal(lnvar, lnvar))
                return nc.vector.tensor_tensor(dest, H, lnvar.unsqueeze(2).to_broadcast([P, NT, F]), ALU.mult)

            dve.wait_ge(sem("y_nodes"), 3)
            layernorm(0, X1).then_inc(sem("h_ready"), 1)

            for l in range(2):
                if l:
                    dve.wait_ge(sem("att_block"), 9 * l)
                link(nc.vector.memset(hTt[0:F + 1, :], 0.0))
                nc.vector.memset(hTt[F:F + 1, :], 1.0).then_inc(sem("hT_cleared"), 1)
                for h in range(HEADS):
                    nc.vector.memset(V[:, :, h, F:F + 1], 1.0).then_inc(sem("ones_set"), 1)
                for b in range(13):
                    n = min(2, NT - 2 * b)
                    dve.wait_ge(sem("v_in_psum"), 13 * l + b + 1)
                    pv = PS[0:P, 2 + b % 4, 0:n * 192].rearrange("p (t c) -> p t c", t=n)
                    for h in range(HEADS):
                        nc.vector.tensor_copy(V[:, 2 * b:2 * b + n, h, 0:F], pv[:, :, F * h:F * h + F]).then_inc(sem("v_copied"), 1)
                    nc.vector.tensor_copy(SK[:, 2 * b:2 * b + n, :], pv[:, :, 128:192]).then_inc(sem("v_copied"), 1)

                def running(c, i):
                    n = l * ATT + c * NT + i
                    if i == 0:
                        dve.wait_ge(sem("max_moved"), l * NC + c)
                        nc.vector.tensor_copy(RM, Tt[:, 0]).then_inc(sem("max_run"), 1)
                    else:
                        dve.wait_ge(sem("max_run"), n)
                        nc.vector.tensor_tensor(RM, RM, Tt[:, i], ALU.max).then_inc(sem("max_run"), 1)

                def log_mask(c, i):
                    n = l * ATT + c * NT + i
                    dve.wait_ge(sem("logged"), n + 1)
                    nc.vector.scalar_tensor_tensor(Lb[i % RING], Cb[i % RING], BIG, Lb[i % RING], ALU.mult, ALU.min
                                                   ).then_inc(sem("masked"), 1)

                def score(c, i):
                    n = l * ATT + c * NT + i
                    dve.wait_ge(sem("masked"), n + 1)
                    dve.wait_ge(sem("scores_in_psum"), n + 1)
                    if not (isinstance(c, int) and c == 0):
                        dve.wait_ge(sem("weighted_sums"), n - NT + 1)
                    s = 2 * (i % 2)
                    nc.vector.tensor_tensor(Tt[:, i], PS[0:P, s:s + 2, 0:D], Lb[i % RING].unsqueeze(1).to_broadcast([P, HEADS, D]),
                                            ALU.add).then_inc(sem("scored"), 1)
                    dve.wait_ge(sem("scored"), n + 1)
                    dve.sem_inc(sem("log_ready"), 1)

                def stage_att(c):
                    for i in range(NT + 2):
                        if i < NT:
                            log_mask(c, i)
                        if i >= 2:
                            score(c, i - 2)
                            running(c, i - 2)
                    dve.wait_ge(sem("max_moved"), l * NC + c + 1)
                    for b in range(3):
                        n = min(4, 10 - 4 * b)
                        nc.vector.tensor_reduce(mrow[:, 4 * b:4 * b + n], PS[0:DB, b, 0:n * P].rearrange("p (a b) -> p a b", a=n), AX, ALU.max
                                                ).then_inc(sem("max_reduced"), 1)
                    dve.wait_ge(sem("max_reduced"), 3 * (l * NC + c) + 3)
                    nc.vector.tensor_scalar(mrow, mrow, FLOOR, None, ALU.max).then_inc(sem("max_ready"), 1)

                stage_att(0)
                with dve.Fori(1, NC) as c:
                    stage_att(c)

                dve.wait_ge(sem("att_copied"), 9 * (l + 1))
                link(nc.vector.tensor_scalar(rec, NDn[:, :, :, F], 1e-16, None, ALU.add))
                link(nc.vector.reciprocal(rec, rec))
                link(nc.vector.tensor_tensor(att, NDn.rearrange("p t h c -> p (t h) c")[:, :, 0:F],
                                             rec.rearrange("p t h -> p (t h)").unsqueeze(2).to_broadcast([P, NT * HEADS, F]), ALU.mult))
                link(nc.vector.tensor_tensor(H, att4[:, :, 0, :], att4[:, :, 1, :], ALU.add))
                ins = nc.vector.scalar_tensor_tensor(H, H, 0.5, SK, ALU.mult, ALU.add)
                if l == 0:
                    link(ins)
                    dve.sem_inc(sem("h_ready"), 1)
                else:
                    link(ins)
            link(nc.vector.tensor_tensor(H, H, X1, ALU.add))
            layernorm(1, H).then_inc(sem("result_ready"), 1)

        @block.tensor
        def _(pe):
            lin_n = [0]

            def lin(w, v):
                pe.wait_ge(sem("lin_used"), lin_n[0])
                lin_n[0] += 1
                for a in range(5):
                    ins = nc.tensor.matmul(PS[:, a, 0:LC], BD[:, w, :], v[:, a * LC:(a + 1) * LC], start=True, stop=True)
                ins.then_inc(sem("lin_done"), 1)

            pe.wait_ge(sem("ident_ready"), 1)
            pe.wait_ge(sem("x_loaded"), 32)
            pe.wait_ge(sem("pad_zeroed"), 1)

            def to_features(a, name):
                for j in range(HALF):
                    ins = nc.tensor.transpose(block_at[j], a[:, j, :, :].rearrange("p h f -> p (h f)"), ident[0:P, 0:P])
                ins.then_inc(sem(name), 1)

            def to_nodes(a, name):
                for j in range(HALF):
                    ins = nc.tensor.transpose(node_at[j], a[:, j * P:(j + 1) * P], ident[:, :])
                ins.then_inc(sem(name), 1)

            to_features(X, "x_blocks")
            pe.wait_ge(sem("weights_loaded"), 16 * 22)
            for i in range(9):
                ins = nc.tensor.transpose(PS[:, 4 + i // 4, (i % 4) * 128:(i % 4 + 1) * 128], BDraw[:, i, :], ident[:, :])
            ins.then_inc(sem("bd_in_psum"), 1)
            pe.wait_ge(sem("watt_loaded"), 16)
            nc.tensor.transpose(PS[0:R, 7, 0:F], Watt, ident[0:F, 0:F]).then_inc(sem("watt_in_psum"), 1)
            pe.wait_ge(sem("bd_ready"), 2)
            pe.wait_ge(sem("ssp_done"), 1)
            lin(1, XA)
            pe.wait_ge(sem("ssp_done"), 2)
            to_nodes(XJ, "xj_in_psum")
            pe.wait_ge(sem("xj_part"), 4)
            lin(0, XA)

            pe.wait_ge(sem("lin_used"), 2)
            pe.wait_ge(sem("ident16_ready"), 1)
            pe.wait_ge(sem("wattT_copied"), 1)

            def edge_group(g, u, k):
                pe.wait_ge(sem("staged"), g + 1)
                pe.wait_ge(sem("matched"), 4 * g)
                for key, bank in ((srch, 0), (dsth, 2)):
                    for s in range(G):
                        ins = nc.tensor.matmul(PS[0:P, bank + s // 4, (s % 4) * P:(s % 4 + 1) * P],
                                               key[:, s:s + 1].to_broadcast([P, P]), identh[0:P, 0:P], start=True, stop=True)
                ins.then_inc(sem("keys_in_psum"), 1)
                pe.wait_ge(sem(f"f_loaded{u}"), 16 * (k + 1))
                pe.wait_ge(sem("fT_copied"), g)
                nc.tensor.transpose(PS[:, 4, 0:P], f8[u], ident[0:P, 0:P]).then_inc(sem("fT_in_psum"), 1)
                pe.wait_ge(sem("fT_copied"), g + 1)
                pe.wait_ge(sem("messages"), g)
                nc.tensor.matmul(PS[0:P, 5, :], fT, Wblk, start=True, stop=True).then_inc(sem("g_in_psum"), 1)
                pe.wait_ge(sem("matched"), 4 * g + 4)
                pe.wait_ge(sem("messages"), g + 1)
                pe.wait_ge(sem("combined"), g)
                for s in range(G):
                    ins = nc.tensor.matmul(PS[0:P, 6, s * F:(s + 1) * F], SelS[:, s, :], msg[:, s, :], start=True, stop=True)
                ins.then_inc(sem("comb_in_psum"), 1)

            pe.wait_ge(sem("wblk_ready"), 16 * G)
            for u in range(2):
                edge_group(u, u, 0)
            with pe.Fori(1, NG // 2) as k:
                for u in range(2):
                    edge_group(2 * k + u, u, k)

            pe.wait_ge(sem("sums_ready"), 1)
            to_features(AGG, "sum_blocks")
            for k in range(3):
                pe.wait_ge(sem("m_updated"), 1 + k)
                lin(3 + k, M)
                pe.wait_ge(sem("ssp_done"), 4 + k)
                lin(6 + k, XA)
            pe.wait_ge(sem("ssp_done"), 7)
            lin(2, XA)
            pe.wait_ge(sem("y_ready"), 1)
            to_nodes(Z, "y_in_psum")

            pe.wait_ge(sem("layer_weights"), 16 * 16)
            for l in range(2):
                Hin = X1 if l == 0 else H
                pe.wait_ge(sem("h_ready"), l + 1)
                for b in range(7):
                    n = min(4, NT - 4 * b)
                    for t in range(n):
                        ins = nc.tensor.transpose(PS[0:F, b, t * P:(t + 1) * P], Hin[:, 4 * b + t, :], ident[0:P, 0:P])
                    ins.then_inc(sem("h_block"), 1)
                pe.wait_ge(sem("hT_copied"), 7 * (l + 1))
                hv = hT[:, 0:N].rearrange("c (p t) -> c t p", t=NT)

                def qk(c, w, bank, n):
                    pe.wait_ge(sem("qk_copied"), max(n - 1, 0))
                    nc.tensor.matmul(PS[:, bank, 0:D], w, hT[:, c * D:(c + 1) * D], start=True, stop=True).then_inc(sem("qk_in_psum"), 1)

                def values(b):
                    n = min(2, NT - 2 * b)
                    v = 13 * l + b
                    pe.wait_ge(sem("v_copied"), 3 * max(v - 3, 0))
                    for t in range(n):
                        ins = nc.tensor.matmul(PS[0:P, 2 + b % 4, t * 192:(t + 1) * 192], hv[:, 2 * b + t, :], wv_(l), start=True, stop=True)
                    ins.then_inc(sem("v_in_psum"), 1)

                for c in range(NC):
                    qk(c, wq_(l), 0, 2 * NC * l + 2 * c)
                    qk(c, wk_(l), 1, 2 * NC * l + 2 * c + 1)
                    values(c)
                for b in range(NC, 13):
                    values(b)
                pe.wait_ge(sem("qk_copied"), 2 * NC * (l + 1))
                pe.wait_ge(sem("v_copied"), 39 * (l + 1))
                pe.wait_ge(sem("ones_set"), 2 * (l + 1))

                def scores(c, i):
                    n = l * ATT + c * NT + i
                    pe.wait_ge(sem("scored"), n if i == 0 else n - 1)
                    for h in range(HEADS):
                        ins = nc.tensor.matmul(PS[0:P, 2 * (i % 2) + h, 0:D], kT[64 * h:64 * h + 64, i, 0:P], qc[64 * h:64 * h + 64, :],
                                               start=True, stop=True)
                    ins.then_inc(sem("scores_in_psum"), 1)

                def weighted(c, i):
                    n = l * ATT + c * NT + i
                    pe.wait_ge(sem("weighed"), n + 1)
                    if i == 0:
                        pe.wait_ge(sem("attended"), 2 * (l * NC + c))
                    for h in range(HEADS):
                        ins = nc.tensor.matmul(PS[0:VW, 4 + h, 0:D], V[:, i, h, :], Tt[:, i, h, :], start=i == 0, stop=i == NT - 1)
                    ins.then_inc(sem("weighted_sums"), 1)

                def stage_att(c, first, last):
                    if not last:
                        pe.wait_ge(sem("qc_ready"), l * NC + c + 1)
                        if not (isinstance(c, int) and l == 0 and c == 0):
                            pe.wait_ge(sem("max_reduced"), 3 * (l * NC + c))
                    for i in range(NT + 1):
                        if i >= 1 and not first:
                            weighted(c - 1, i - 1)
                        if i < NT and not last:
                            scores(c, i)
                    if last:
                        return
                    pe.wait_ge(sem("scored"), l * ATT + (c + 1) * NT)
                    pe.wait_ge(sem("max_run"), l * ATT + (c + 1) * NT)
                    for b in range(10):
                        ins = nc.tensor.transpose(PS[0:DB, b // 4, (b % 4) * P:(b % 4 + 1) * P],
                                                  RM[:, b // 5, (b % 5) * DB:(b % 5 + 1) * DB], ident[0:P, 0:P])
                    ins.then_inc(sem("max_moved"), 1)
                    pe.wait_ge(sem("max_ready"), l * NC + c + 1)
                    pe.wait_ge(sem("max_spread"), l * NC + c)
                    for b in range(10):
                        ins = nc.tensor.matmul(PS[0:P, 6 + b // 5, (b % 5) * DB:(b % 5 + 1) * DB], mrow[:, b:b + 1].to_broadcast([DB, P]),
                                               ident[0:DB, 0:DB], start=True, stop=True)
                    ins.then_inc(sem("max_in_psum"), 1)

                stage_att(0, True, False)
                with pe.Fori(1, NC) as c:
                    stage_att(c, False, False)
                stage_att(NC, False, True)
                pe.wait_ge(sem("attended"), 2 * NC * (l + 1))
                ov = [OT[h][:, 0:N].rearrange("c (p t) -> c t p", t=NT) for h in range(HEADS)]
                for b in range(9):
                    n = min(3, NT - 3 * b)
                    if b == 8:
                        pe.wait_ge(sem("att_copied"), 9 * l + 1)
                    for t in range(n):
                        for h in range(HEADS):
                            ins = nc.tensor.transpose(PS[0:P, b % 8, (2 * t + h) * VW:(2 * t + h + 1) * VW], ov[h][:, 3 * b + t, :],
                                                      ident[0:VW, 0:VW])
                    ins.then_inc(sem("att_block"), 1)


_INS = ['x', 'src', 'dst', 'edge_attr_16', 'L0_gnn_W_att', 'L0_gnn_W_i', 'L0_gnn_b_i', 'L0_gnn_W_j', 'L0_gnn_b_j', 'L0_gnn_W_v', 'L0_gnn_b_v', 'L0_gnn_res_dense_W', 'L0_gnn_res_dense_b', 'L0_gnn_res_res_W', 'L0_gnn_res_res_b', 'L0_gnn_gate', 'L1_gnn_l1_wq', 'L1_gnn_l1_bq', 'L1_gnn_l1_wk', 'L1_gnn_l1_bk', 'L1_gnn_l1_wv', 'L1_gnn_l1_bv', 'L1_gnn_l1_ws', 'L1_gnn_l1_bs', 'L1_gnn_l2_wq', 'L1_gnn_l2_bq', 'L1_gnn_l2_wk', 'L1_gnn_l2_bk', 'L1_gnn_l2_wv', 'L1_gnn_l2_bv', 'L1_gnn_l2_ws', 'L1_gnn_l2_bs']
_OUTS = [((3125, 64), 'float32')]


def kernel(**inputs):
    import numpy as _np
    import concourse.bacc as _bacc
    from concourse import mybir as _mybir
    from concourse.bass_utils import run_bass_kernel_spmd as _run

    nc = _bacc.Bacc("TRN2", target_bir_lowering=False, num_devices=1)
    arrays, args = {}, []
    for name in _INS:
        a = _np.ascontiguousarray(inputs[name])
        arrays[f"in_{name}_dram"] = a
        args.append(nc.dram_tensor(f"in_{name}_dram", a.shape, _mybir.dt.from_np(a.dtype), kind="ExternalInput").ap())
    for i, (shape, dtype) in enumerate(_OUTS):
        dt = _mybir.dt.from_np(_np.dtype(dtype))
        args.append(nc.dram_tensor(f"out_{i}_dram", shape, dt, kind="ExternalOutput").ap())
    build(nc, *args)
    r = _run(nc, [arrays], core_ids=[0])
    return r.results[0]["out_0_dram"]
```

```python
from contextlib import ExitStack

import concourse.bass as bass
from concourse import mybir

N = 3125
E = 100000
F = 64
R = 16
P = 125
NT = N // P
EJ = E // P
G = 8
NG = EJ // G
HALF = (NT + 1) // 2
HC = HALF * P
LC = HC // 5
BLK = 2
D = BLK * P
NC = -(-NT // BLK)
ND = NC * D
QC = ND // 10
RING = 5
BANKS = 6
LAG = 3
ACCS = G
BIG = 1e30
FLOOR = -1e20
HEADS = 2
EXP_LN_SET = 6
VW = F + 1
ATT = NC * NT


def build(nc, x, src, dst, edge_attr, W_att, W_i, b_i, W_j, b_j, W_v, b_v, rd_W, rd_b, rr_W, rr_b, gate,
          wq1, bq1, wk1, bk1, wv1, bv1, ws1, bs1, wq2, bq2, wk2, bk2, wv2, bv2, ws2, bs2, out):
    f32 = mybir.dt.float32
    f16 = mybir.dt.float16
    i32 = mybir.dt.int32
    ALU = mybir.AluOpType
    ACT = mybir.ActivationFunctionType
    AX = mybir.AxisListType.X
    layers = [(wq1, bq1, wk1, bk1, wv1, bv1, ws1, bs1), (wq2, bq2, wk2, bk2, wv2, bv2, ws2, bs2)]

    xj_dram = nc.dram_tensor("xj_rows", [N, F], f32, kind="Internal").ap()
    acc_dram = [nc.dram_tensor(f"message_sums{u}", [N + P, F], f32, kind="Internal").ap() for u in range(ACCS)]
    cnt_dram = nc.dram_tensor("edge_counts", [N * ND + P, 1], f32, kind="Internal").ap()
    cnt_rows = cnt_dram[0:N * ND, :].rearrange("(t p d) o -> p t (d o)", p=P, t=NT)
    log_dram = nc.dram_tensor("log_counts", [NT, P, ND], f32, kind="Internal").ap()

    ctx = ExitStack()
    with ctx:
        ctx.enter_context(nc.allow_non_contiguous_dma(reason="short bias columns"))

        def sb(name, cols, dt=f32):
            return ctx.enter_context(nc.sbuf_tensor(name, [128, cols], dt))

        sems = {}

        def sem(name):
            if name not in sems:
                sems[name] = ctx.enter_context(nc.semaphore(name))
            return sems[name]

        T = sb("scores", 2 * NT * HEADS * D)
        Xt = sb("x_nodes", (NT + 1) * F)
        X1t = sb("x1_nodes", NT * F)
        Ht = sb("h_nodes", NT * F)
        SKt = sb("skip_nodes", NT * F)
        hTt = sb("h_features", ND)
        qTt = sb("q_features", ND)
        kTt = sb("k_features", ND)
        Vt = sb("v_nodes", NT * HEADS * VW)
        O1t = sb("attended1", ND)
        Rt = sb("running_max", HEADS * D)
        MBt = sb("max_of_targets", HEADS * D)
        CL = sb("counts_and_logs", 2 * RING * D)
        qct = sb("q_chunk", HEADS * D)
        WL = sb("layer_weights", 2 * (128 + 128 + 192))
        BC = sb("bias_columns", 12)
        ident = sb("identity", 128)
        identh = sb("identity16", 128, f16)
        small = sb("small", 192)
        halfc = sb("half_column", 1)
        kh = sb("keys16", 2 * G, f16)
        PS = ctx.enter_context(nc.psum_tensor("PS", [128, 8, 512], f32))

        def grid(t, a, off=0, b=None, parts=128):
            return t[0:parts, off:off + a * b].rearrange("p (a b) -> p a b", b=b)

        X = Xt[0:P, :].rearrange("p (j h f) -> p j h f", h=2, f=F)
        X1 = grid(X1t, NT, 0, F, P)
        H = grid(Ht, NT, 0, F, P)
        SK = grid(SKt, NT, 0, F, P)
        BD = grid(SKt, 9, 0, 128)
        BDraw = grid(T, 9, 0, 128)
        xT2 = O1t[:, 0:HC]
        M = kTt[:, 0:HC]
        Z = qTt[:, 0:HC]
        LG = Vt[:, 0:HC]
        XA = hTt[:, 0:HC]
        XJ = T[:, 1200:1200 + HC]
        XJn = grid(T, NT + 1, 3000, F, P)
        zero_tile = T[0:P, 5000:5000 + 26 * F]
        cfill = T[0:P, 21000:21000 + ND]

        at = [7000]

        def take(n):
            at[0] += n
            return at[0] - n

        o = take(EJ)
        src_i = T[0:P, o:o + EJ].bitcast(i32)
        o = take(EJ)
        dst_i = T[0:P, o:o + EJ].bitcast(i32)
        SelS = grid(T, G, take(G * P), P, P)
        SelD = grid(T, G, take(G * P), P, P)
        SelP = grid(T, G, take(G * P), P, P)
        tmpP = grid(T, G, take(G * P), P, P)
        tmpS = grid(T, G, take(G * P), P, P)
        gx = [T[0:P, o:o + G * F] for o in (take(G * F), take(G * F))]
        msg = grid(T, G, take(G * F), F, P)
        cm = [T[0:P, o:o + G * F] for o in (take(G * F), take(G * F))]
        f8 = [T[0:P, o:o + G * R] for o in (take(G * R), take(G * R))]
        o = take(P)
        fT = T[:, o:o + P]
        o = take(G * F)
        Wblk = T[:, o:o + G * F]
        o = take(P)
        low = T[0:P, o:o + P]
        o = take(R)
        Watt = T[0:F, o:o + R]
        o = take(F)
        WattT = T[0:R, o:o + F]
        assert at[0] <= 21000
        sc = [0]

        def col(n, parts=P):
            sc[0] += n
            assert sc[0] <= 160
            return small[0:parts, sc[0] - n:sc[0]]

        srcf, dstf, tS, tC, base, sumC, preS, preP = (col(G) for _ in range(8))
        dcur = [col(G).bitcast(i32) for _ in range(2)]
        sidx = [col(G).bitcast(i32) for _ in range(2)]
        cidx = [col(G).bitcast(i32) for _ in range(2)]
        cnt = [col(G) for _ in range(2)]
        trash_i = col(2).bitcast(i32)
        trash = col(2)
        srch, dsth = kh[0:P, 0:G], kh[0:P, G:2 * G]

        ACC = [grid(T, NT, u * NT * F, F, P) for u in range(ACCS)]
        AGG = X

        Tt = T[0:P, :].rearrange("p (b i h d) -> p b i h d", b=2, i=NT, h=HEADS)
        RM = Rt[0:P, :].rearrange("p (h d) -> p h d", h=HEADS)
        MB = MBt[0:P, :].rearrange("p (h d) -> p h d", h=HEADS)
        Cb = [CL[0:P, r * D:(r + 1) * D] for r in range(RING)]
        Lb = [CL[0:P, (RING + r) * D:(RING + r + 1) * D] for r in range(RING)]
        hT = hTt[0:F + 1, :]
        qT, kT, qc = qTt[:, :], kTt[:, :], qct[:, :]
        V = Vt[0:P, :].rearrange("p (t h c) -> p t h c", t=NT, h=HEADS)
        AO = [hTt[0:VW, :], O1t[0:VW, :]]
        mrow = small[0:P, 160:160 + BLK * HEADS]
        NDn = T[0:P, 0:NT * HEADS * VW].rearrange("p (t h c) -> p t h c", t=NT, h=HEADS)
        rec = T[0:P, 4000:4000 + NT * HEADS].rearrange("p (t h) -> p t h", t=NT)
        att = grid(T, NT * HEADS, 5000, F, P)
        att4 = T[0:P, 5000:5000 + NT * HEADS * F].rearrange("p (t h c) -> p t h c", t=NT, h=HEADS)
        lnsum, lnvar = T[0:P, 9000:9000 + NT], T[0:P, 9100:9100 + NT]
        lnsq = grid(T, NT, 10000, F, P)

        def wq_(l):
            return WL[0:F + 1, l * 448:l * 448 + 128]

        def wk_(l):
            return WL[0:F + 1, l * 448 + 128:l * 448 + 256]

        def wv_(l):
            return WL[0:F + 1, l * 448 + 256:l * 448 + 448]

        pairs = [PS[:, 0:3, 0:500], PS[:, 3:4, 0:P]]
        block_at = [PS[:, j // 4, (j % 4) * P:(j % 4 + 1) * P] for j in range(HALF)]
        node_at = [PS[0:P, j // 4, (j % 4) * 128:(j % 4 + 1) * 128] for j in range(HALF)]
        score_ring = [PS[0:P, r, 0:HEADS * D] for r in range(BANKS)]
        lin5 = PS[:, 0:5, 0:LC]

        def product(stage, a):
            return PS[:, (5 * stage + a) % 8, 0:LC]

        def cols(v, a):
            return v[:, a * LC:(a + 1) * LC]


        def five(v):
            return v.rearrange("p (a b) -> p a b", a=5)

        fe = edge_attr.rearrange("(p j) r -> p (j r)", p=P)

        block = ctx.enter_context(nc.Block())

        @block.sync
        def _(sp):
            xv = x.rearrange("(t p) f -> p t f", p=P)
            sp.dma_start(X[:, :, 0, :], xv[:, 0:HALF, :]).then_inc(sem("x_loaded"), 16)
            sp.dma_start(X[:, 0:NT - HALF, 1, :], xv[:, HALF:NT, :]).then_inc(sem("x_loaded"), 16)
            sp.wait_ge(sem("bd_zeroed"), 1)
            for h in range(2):
                q = slice(64 * h, 64 * h + 64)
                for i, w in enumerate((W_i, W_j, W_v)):
                    sp.dma_start(BDraw[q, i, q], w).then_inc(sem("weights_loaded"), 16)
                for i, w in ((3, rd_W), (6, rr_W)):
                    sp.dma_start(BDraw[q, i:i + 3, q], w.rearrange("k g f -> g k f")).then_inc(sem("weights_loaded"), 16)
                for i, b in enumerate((b_i, b_j, b_v, gate)):
                    sp.dma_start(BC[q, i:i + 1], b.rearrange("(f o) -> f o", o=1)).then_inc(sem("weights_loaded"), 16)
                for i, b in ((4, rd_b), (7, rr_b)):
                    sp.dma_start(BC[q, i:i + 3], b.rearrange("k f -> f k")).then_inc(sem("weights_loaded"), 16)
            sp.dma_start(Watt, W_att).then_inc(sem("watt_loaded"), 16)
            sp.dma_start(src_i, src.rearrange("(p j) -> p j", p=P)).then_inc(sem("edges_loaded"), 16)
            sp.dma_start(dst_i, dst.rearrange("(p j) -> p j", p=P)).then_inc(sem("edges_loaded"), 16)
            sp.wait_ge(sem("fills_set"), 2)
            for u in range(ACCS):
                sp.dma_start(acc_dram[u].rearrange("(p t) f -> p (t f)", p=P), zero_tile).then_inc(sem("sums_cleared"), 16)
            for t in range(NT):
                if t == 5:
                    sp.wait_ge(sem("xj_stored"), 16)
                    for u in range(2):
                        sp.wait_ge(sem(f"f_loaded{u}"), 16)
                sp.dma_start(cnt_rows[:, t, :], cfill).then_inc(sem("counts_cleared"), 16)
            sp.dma_start(cnt_dram[N * ND:N * ND + P, :], cfill[:, 0:1]).then_inc(sem("counts_cleared"), 16)
            for l, (wq, bq, wk, bk, wv, bv, ws, bs) in enumerate(layers):
                for w, b, dest in ((wq, bq, wq_(l)), (wk, bk, wk_(l)), (wv, bv, wv_(l)[:, 0:128]), (ws, bs, wv_(l)[:, 128:192])):
                    sp.dma_start(dest[0:F, :], w).then_inc(sem("layer_weights"), 16)
                    sp.dma_start(dest[F:F + 1, :], b.rearrange("(o f) -> o f", o=1)).then_inc(sem("layer_weights"), 16)
            def load_f(g, u):
                sp.wait_ge(sem("fT_in_psum"), g - 1)
                sp.dma_start(f8[u], fe[:, bass.ds(g * (G * R), G * R)]).then_inc(sem(f"f_loaded{u}"), 16)

            with sp.Fori(1, NG // 2) as k:
                for u in range(2):
                    load_f(2 * k + u, u)

            for u in range(ACCS):
                sp.wait_ge(sem(f"sum_added{u}"), 16 * NG)
                sp.dma_start(ACC[u], acc_dram[u][0:N, :].rearrange("(t p) f -> p t f", p=P)).then_inc(sem(f"sums_loaded{u}"), 16)

            sp.wait_ge(sem("count_added"), 16 * EJ)
            for l in range(2):
                if l:
                    for r in range(RING):
                        sp.wait_ge(sem(f"log_stored{r}"), 16 * ATT // RING)

                def settled():
                    sp.sem_inc(sem("sync_waited"), 1)

                def load(c, i):
                    n = l * ATT + c * NT + i
                    r = i % RING
                    if not (isinstance(n, int) and n < RING):
                        sp.wait_ge(sem("scored"), n - RING + 1)
                        settled()
                        if l == 0:
                            sp.wait_ge(sem(f"log_stored{r}"), 16 * (NT // RING) * c + 16 * (i // RING))
                        settled()
                    src_rows = log_dram.rearrange("t p d -> p t d") if l else cnt_rows
                    sp.dma_start(Cb[r], src_rows[:, i, bass.ds(c * D, D)]).then_inc(sem(f"count_loaded{r}"), 16)

                def store(c, i):
                    n = l * ATT + c * NT + i
                    sp.wait_ge(sem("masked"), n + 1)
                    settled()
                    sp.dma_start(log_dram[i, :, bass.ds(c * D, D)], Cb[i % RING]).then_inc(sem(f"log_stored{i % RING}"), 16)

                def chunk(c):
                    for i in range(NT + 3):
                        if i < NT:
                            load(c, i)
                        if l == 0 and i >= 3:
                            store(c, i - 3)

                chunk(0)
                with sp.Fori(1, NC) as c:
                    chunk(c)
            sp.wait_ge(sem("result_ready"), 1)
            sp.dma_start(out.rearrange("(t p) f -> p t f", p=P), H).then_inc(sem("stored"), 16)
            sp.wait_ge(sem("stored"), 16)

        @block.gpsimd
        def _(pool):
            nc.gpsimd.memset(BDraw, 0.0).then_inc(sem("bd_zeroed"), 1)
            nc.gpsimd.memset(ident[:, :], 0.0).then_inc(sem("ident_zeroed"), 1)
            pool.wait_ge(sem("ident_zeroed"), 1)
            nc.gpsimd.affine_select(out=ident[:, :], in_=ident[:, :], compare_op=ALU.not_equal, fill=1.0, base=0,
                                    pattern=[[-1, 128]], channel_multiplier=1).then_inc(sem("ident_ready"), 1)
            nc.gpsimd.memset(zero_tile, 0.0).then_inc(sem("fills_set"), 1)
            nc.gpsimd.memset(cfill, -0.5).then_inc(sem("fills_set"), 1)
            nc.gpsimd.memset(Wblk, 0.0).then_inc(sem("wblk_zeroed"), 1)
            nc.gpsimd.memset(low, 1.0).then_inc(sem("low_set"), 1)
            pool.wait_ge(sem("low_set"), 1)
            nc.gpsimd.affine_select(out=low, in_=low, compare_op=ALU.is_gt, fill=0.0, base=0,
                                    pattern=[[-1, P]], channel_multiplier=1).then_inc(sem("low_ready"), 1)
            nc.gpsimd.iota(trash_i[:, 0:1], pattern=[[0, 1]], base=N, channel_multiplier=1).then_inc(sem("trash_iota"), 1)
            nc.gpsimd.iota(trash_i[:, 1:2], pattern=[[0, 1]], base=N * ND, channel_multiplier=1).then_inc(sem("trash_iota"), 1)

            def settled():
                pool.sem_inc(sem("pool_waited"), 1)

            def gather(g, u, s):
                pool.indirect_dma_start(gx[u][:, s * F:(s + 1) * F], None, xj_dram,
                                        bass.IndirectOffsetOnAxis(ap=dcur[u][:, s:s + 1], axis=0)
                                        ).then_inc(sem(f"gathered{u}"), 16)

            def scatter(g, u, s):
                pool.wait_ge(sem(f"sum_added{s}"), 16 * g)
                settled()
                pool.indirect_dma_start(acc_dram[s], bass.IndirectOffsetOnAxis(ap=sidx[u][:, s:s + 1], axis=0),
                                        cm[u][:, s * F:(s + 1) * F], None, compute_op=ALU.add
                                        ).then_inc(sem(f"sum_added{s}"), 16)
                pool.wait_ge(sem("count_added"), 16 * G * g + 16 * s)
                settled()
                pool.indirect_dma_start(cnt_dram, bass.IndirectOffsetOnAxis(ap=cidx[u][:, s:s + 1], axis=0),
                                        cnt[u][:, s:s + 1], None, compute_op=ALU.add
                                        ).then_inc(sem("count_added"), 16)

            def group(g, u, gathers, scatters):
                if gathers:
                    pool.wait_ge(sem("targets_staged"), g + 1)
                if scatters:
                    pool.wait_ge(sem("combined"), g - 1)
                    pool.wait_ge(sem("indexed"), g - 1)
                settled()
                for s in range(G):
                    if gathers:
                        gather(g, u, s)
                    if scatters:
                        scatter(g - 2, u, s)

            pool.wait_ge(sem("xj_stored"), 16)
            for u in range(2):
                group(u, u, True, False)
            pool.wait_ge(sem("sums_cleared"), 16 * ACCS)
            pool.wait_ge(sem("counts_cleared"), 16 * (NT + 1))
            for u in range(2):
                group(2 + u, u, True, True)
            with pool.Fori(2, NG // 2) as k:
                for u in range(2):
                    group(2 * k + u, u, True, True)
            for u in range(2):
                group(NG + u, u, False, True)

            for l in range(2):
                def shift(c, b, i):
                    if i == 0:
                        pool.wait_ge(sem("max_spread"), l * NC + c + 1)
                    nc.gpsimd.tensor_tensor(Tt[:, b, i], Tt[:, b, i], MB, ALU.subtract).then_inc(sem("shifted"), 1)

                with pool.Fori(0, NC // 2) as k:
                    for b in range(2):
                        for i in range(NT):
                            shift(2 * k + b, b, i)
                for i in range(NT):
                    shift(NC - 1, 0, i)

        @block.scalar
        def _(act):
            ssp_n, lin_n = [0], [0]

            def load_exp_ln():
                act.add_instruction(mybir.InstLoadActFuncSet(name=nc.get_next_instruction_name(), engine=mybir.EngineType.Activation, act_func_set_id=EXP_LN_SET, ins=[], outs=[]))

            load_exp_ln()

            def ssp(z):
                k = ssp_n[0]
                ssp_n[0] += 1
                act.wait_ge(sem("ssp_done"), k)
                nc.scalar.activation(LG, z, ACT.Abs).then_inc(sem("ssp_abs"), 1)
                act.wait_ge(sem("ssp_abs"), k + 1)
                nc.scalar.activation(LG, LG, ACT.Exp, scale=-1.0).then_inc(sem("ssp_exp"), 1)
                act.wait_ge(sem("ssp_exp"), k + 1)
                nc.scalar.activation(LG, LG, ACT.Ln, scale=0.5, bias=halfc[:, :]).then_inc(sem("ssp_ln"), 1)

            def lin_bias(b):
                lin_n[0] += 1
                act.wait_ge(sem("lin_done"), lin_n[0])
                act.wait_ge(sem("ssp_done"), ssp_n[0])
                nc.scalar.activation(five(Z), lin5, ACT.Identity, bias=BC[:, b:b + 1]).then_inc(sem("lin_used"), 1)
                act.wait_ge(sem("lin_used"), lin_n[0])

            act.wait_ge(sem("x_blocks"), 1)
            nc.scalar.activation(xT2[:, 0:1500].rearrange("p (a b) -> p a b", a=3), pairs[0], ACT.Copy).then_inc(sem("xT_copied"), 1)
            nc.scalar.activation(xT2[:, 1500:HC].rearrange("p (a b) -> p a b", a=1), pairs[1], ACT.Copy).then_inc(sem("xT_copied"), 1)
            act.wait_ge(sem("xT_copied"), 2)
            act.wait_ge(sem("half_set"), 1)
            ssp(xT2)
            act.wait_ge(sem("bd_in_psum"), 1)
            nc.scalar.activation(BD[:, 0:8, :].rearrange("p (a b) c -> p a (b c)", a=2), PS[:, 4:6, :], ACT.Copy).then_inc(sem("bd_ready"), 1)
            nc.scalar.activation(BD[:, 8, :], PS[:, 6, 0:128], ACT.Copy).then_inc(sem("bd_ready"), 1)
            act.wait_ge(sem("watt_in_psum"), 1)
            nc.scalar.activation(WattT, PS[0:R, 7, 0:F], ACT.Copy).then_inc(sem("wattT_copied"), 1)
            lin_bias(1)
            ssp(Z)
            act.wait_ge(sem("xj_in_psum"), 1)
            for h in range(2):
                nc.scalar.activation(XJn[:, HALF * h:HALF * h + 12, :].rearrange("p (a b) f -> p a b f", a=3),
                                     PS[0:P, 0:3, :].rearrange("p a (b h f) -> p a b h f", h=2, f=F)[:, :, :, h, :],
                                     ACT.Copy).then_inc(sem("xj_part"), 1)
                nc.scalar.activation(XJn[:, HALF * h + 12, :], PS[0:P, 3, F * h:F * h + F], ACT.Copy).then_inc(sem("xj_part"), 1)
            act.wait_ge(sem("xj_part"), 4)
            act.dma_start(xj_dram.rearrange("(t p) f -> p t f", p=P), XJn[:, 0:NT, :]).then_inc(sem("xj_stored"), 16)
            act.wait_ge(sem("wblk_zeroed"), 1)
            act.wait_ge(sem("wattT_copied"), 1)
            for j in range(G):
                act.dma_start(Wblk[R * j:R * j + R, F * j:F * j + F], WattT).then_inc(sem("wblk_ready"), 16)
            for u in range(2):
                act.dma_start(f8[u], fe[:, u * G * R:(u + 1) * G * R]).then_inc(sem(f"f_loaded{u}"), 16)
            lin_bias(0)
            ssp(Z)

            def edge_group(g, u, first):
                act.wait_ge(sem("fT_in_psum"), g + 1)
                act.wait_ge(sem("g_in_psum"), g)
                nc.scalar.activation(fT, PS[:, 4, 0:P], ACT.Copy).then_inc(sem("fT_copied"), 1)
                act.wait_ge(sem("comb_in_psum"), g + 1)
                if not first:
                    for s in range(ACCS):
                        act.wait_ge(sem(f"sum_added{s}"), 16 * (g - 1))
                nc.scalar.activation(cm[u], PS[0:P, 6, :], ACT.Copy).then_inc(sem("combined"), 1)

            for u in range(2):
                edge_group(u, u, True)
            with act.Fori(1, NG // 2) as k:
                for u in range(2):
                    edge_group(2 * k + u, u, False)

            for k in range(4):
                for a in range(5):
                    n = 5 * k + a
                    if k < 3:
                        act.wait_ge(sem("block_biased"), n + 1)
                        nc.scalar.activation(cols(LG, a), cols(Z, a), ACT.Abs).then_inc(sem("block_abs"), 1)
                    else:
                        act.wait_ge(sem("residual_added"), 10 + a + 1)
                        nc.scalar.activation(cols(LG, a), cols(M, a), ACT.Abs).then_inc(sem("block_abs"), 1)
                    act.wait_ge(sem("block_abs"), n + 1)
                    nc.scalar.activation(cols(LG, a), cols(LG, a), ACT.Exp, scale=-1.0).then_inc(sem("block_exp"), 1)
                    act.wait_ge(sem("block_exp"), n + 1)
                    nc.scalar.activation(cols(LG, a), cols(LG, a), ACT.Ln, scale=0.5, bias=halfc[:, :]).then_inc(sem("block_ln"), 1)
            act.wait_ge(sem("y_in_psum"), 1)
            for h in range(2):
                nc.scalar.activation(H[:, HALF * h:HALF * h + 12, :].rearrange("p (a b) f -> p a b f", a=3),
                                     PS[0:P, 0:3, :].rearrange("p a (b h f) -> p a b h f", h=2, f=F)[:, :, :, h, :],
                                     ACT.Copy).then_inc(sem("y_nodes"), 1)
            nc.scalar.activation(H[:, 12, :], PS[0:P, 3, 0:F], ACT.Copy).then_inc(sem("y_nodes"), 1)

            def ln_act(k):
                act.wait_ge(sem("ln_centered"), k + 1)
                nc.scalar.activation(lnsq, H, ACT.Square).then_inc(sem("ln_squared"), 1)
                act.wait_ge(sem("ln_var"), k + 1)
                nc.scalar.activation(lnvar, lnvar, ACT.Sqrt).then_inc(sem("ln_std"), 1)

            ln_act(0)
            load_exp_ln()

            for l in range(2):
                act.wait_ge(sem("hT_cleared"), l + 1)
                for b in range(7):
                    n = min(4, NT - 4 * b)
                    act.wait_ge(sem("h_block"), 7 * l + b + 1)
                    nc.scalar.activation(hT[0:F, 4 * b * P:(4 * b + n) * P], PS[0:F, b, 0:n * P], ACT.Copy
                                         ).then_inc(sem("hT_copied"), 1)
                for c in range(10):
                    act.wait_ge(sem("qk_in_psum"), 20 * l + 2 * c + 1)
                    nc.scalar.activation(qT[:, c * QC:(c + 1) * QC], PS[:, 0, 0:QC], ACT.Copy, scale=0.125).then_inc(sem("qk_copied"), 1)
                    act.wait_ge(sem("qk_in_psum"), 20 * l + 2 * c + 2)
                    nc.scalar.activation(kT[:, c * QC:(c + 1) * QC], PS[:, 1, 0:QC], ACT.Copy).then_inc(sem("qk_copied"), 1)

                def logs(c, i):
                    n = c * NT + i
                    act.wait_ge(sem(f"count_loaded{i % RING}"), 16 * (NT // RING) * c + 16 * (i // RING + 1))
                    if not (isinstance(n, int) and n < RING):
                        act.wait_ge(sem("masked"), n - RING + 1)
                    nc.scalar.activation(Lb[i % RING], Cb[i % RING], ACT.Abs).then_inc(sem("magnitude"), 1)
                    act.wait_ge(sem("magnitude"), n + 1)
                    nc.scalar.activation(Lb[i % RING], Lb[i % RING], ACT.Ln, bias=halfc[0:P, :]).then_inc(sem("logged"), 1)

                def exps(c, b, i):
                    n = l * ATT + c * NT + i
                    act.wait_ge(sem("shifted"), n + 1)
                    nc.scalar.activation(Tt[:, b, i], Tt[:, b, i], ACT.Exp).then_inc(sem("weighed"), 1)

                def stage(c, b, first, last):
                    if not last:
                        if not (isinstance(c, int) and l == 0 and c == 0):
                            act.wait_ge(sem("scores_in_psum"), l * ATT + c * NT)
                        if isinstance(c, int) and c == 0:
                            act.wait_ge(sem("qk_copied"), 20 * (l + 1))
                            act.wait_ge(sem("qc_zeroed"), 1)
                        for h in range(HEADS):
                            nc.scalar.activation(qc[F * h:F * h + F, h * D:h * D + D], qT[F * h:F * h + F, bass.ds(c * D, D)], ACT.Copy
                                                 ).then_inc(sem("qc_ready"), 1)
                    if not last and l == 0:
                        for i in range(LAG):
                            logs(c, i)
                    if not first:
                        act.wait_ge(sem("max_in_psum"), l * NC + c)
                        nc.scalar.activation(MB, PS[0:P, 7, 0:HEADS * D].rearrange("p (h d) -> p h d", h=HEADS), ACT.Copy).then_inc(sem("max_spread"), 1)
                    for i in range(NT):
                        if not first:
                            exps(c - 1, 1 - b, i)
                        if not last and l == 0 and i + LAG < NT:
                            logs(c, i + LAG)
                    if not first:
                        act.wait_ge(sem("weighted_sums"), l * ATT + c * NT)
                        for h in range(HEADS):
                            nc.scalar.activation(AO[h][:, bass.ds((c - 1) * D, D)], PS[0:VW, 6, h * D:(h + 1) * D], ACT.Copy
                                                 ).then_inc(sem("attended"), 1)

                if l == 0:
                    act.sem_inc(sem("attended"), 2)
                stage(0, 0, True, False)
                with act.Fori(0, NC // 2) as k:
                    stage(2 * k + 1, 1, False, False)
                    stage(2 * k + 2, 0, False, False)
                stage(NC, 1, False, True)
                for b in range(9):
                    n = min(3, NT - 3 * b)
                    act.wait_ge(sem("att_block"), 9 * l + b + 1)
                    nc.scalar.activation(NDn[:, 3 * b:3 * b + n].rearrange("p t h c -> p (t h c)"), PS[0:P, b % 6, 0:n * HEADS * VW], ACT.Copy
                                         ).then_inc(sem("att_copied"), 1)
            ln_act(1)

        @block.vector
        def _(dve):
            ssp_n, lin_n = [0], [0]

            def ssp(z, dest):
                ssp_n[0] += 1
                dve.wait_ge(sem("ssp_ln"), ssp_n[0])
                nc.vector.scalar_tensor_tensor(dest, z, 0.0, LG, ALU.max, ALU.add).then_inc(sem("ssp_done"), 1)

            chain = [0]

            def link(ins):
                chain[0] += 1
                ins.then_inc(sem("vector_chain"), 1)
                dve.wait_ge(sem("vector_chain"), chain[0])

            nc.vector.memset(qc, 0.0).then_inc(sem("qc_zeroed"), 1)
            nc.vector.memset(halfc[:, :], 0.5).then_inc(sem("half_set"), 1)
            nc.vector.memset(X[:, HALF - 1, 1, :], 0.0).then_inc(sem("pad_zeroed"), 1)
            dve.wait_ge(sem("ident_ready"), 1)
            nc.vector.tensor_copy(identh[:, :], ident[:, :]).then_inc(sem("ident16_ready"), 1)
            dve.wait_ge(sem("trash_iota"), 2)
            nc.vector.tensor_copy(trash, trash_i).then_inc(sem("trash_ready"), 1)
            dve.wait_ge(sem("trash_ready"), 1)
            dve.wait_ge(sem("edges_loaded"), 32)

            def stage_targets(g, u):
                nc.vector.tensor_copy(dcur[u], dst_i[:, bass.ds(g * G, G)]).then_inc(sem("targets_staged"), 1)

            def stage(g):
                sl = bass.ds(g * G, G)
                nc.vector.tensor_copy(srcf, src_i[:, sl]).then_inc(sem("keys_copied"), 1)
                nc.vector.tensor_copy(dstf, dst_i[:, sl]).then_inc(sem("keys_copied"), 1)
                nc.vector.tensor_scalar(srch, src_i[:, sl], float(-(N // 2)), None, ALU.add).then_inc(sem("keys_copied"), 1)
                nc.vector.tensor_scalar(dsth, dst_i[:, sl], float(-(N // 2)), None, ALU.add).then_inc(sem("keys_copied"), 1)
                dve.wait_ge(sem("keys_copied"), 4 * g + 4)
                dve.sem_inc(sem("staged"), 1)

            def compute(g, u, k, first, last):
                if not last:
                    stage_targets(g + 1, 1 - u)
                dve.wait_ge(sem("keys_in_psum"), g + 1)
                dve.wait_ge(sem("comb_in_psum"), g)
                for b in range(2):
                    q = slice(4 * b, 4 * b + 4)
                    for key, sel, bank in ((srch, SelS, b), (dsth, SelD, 2 + b)):
                        nc.vector.tensor_tensor(sel[:, q, :], PS[0:P, bank, 0:4 * P].rearrange("p (a b) -> p a b", a=4),
                                                key[:, q].unsqueeze(2).to_broadcast([P, 4, P]), ALU.is_equal
                                                ).then_inc(sem("matched"), 1)
                dve.wait_ge(sem("matched"), 4 * g + 4)
                nc.vector.tensor_tensor(SelP, SelS, SelD, ALU.mult).then_inc(sem("pairs"), 1)
                lowb = low.unsqueeze(1).to_broadcast([P, G, P])
                nc.vector.tensor_tensor(tmpS, SelS, lowb, ALU.mult).then_inc(sem("before_s"), 1)
                dve.wait_ge(sem("pairs"), g + 1)
                nc.vector.tensor_tensor(tmpP, SelP, lowb, ALU.mult).then_inc(sem("before_p"), 1)
                if not first:
                    dve.wait_ge(sem("count_added"), 16 * G * (g - 1))
                    for s in range(ACCS):
                        dve.wait_ge(sem(f"sum_added{s}"), 16 * (g - 1))
                nc.vector.tensor_reduce(cnt[u], SelP, AX, ALU.add).then_inc(sem("counted"), 1)
                dve.wait_ge(sem("before_s"), g + 1)
                nc.vector.tensor_reduce(preS, tmpS, AX, ALU.add).then_inc(sem("earlier"), 1)
                dve.wait_ge(sem("before_p"), g + 1)
                nc.vector.tensor_reduce(preP, tmpP, AX, ALU.add).then_inc(sem("earlier"), 1)
                nc.vector.scalar_tensor_tensor(base, srcf, float(ND), dstf, ALU.mult, ALU.add).then_inc(sem("cells"), 1)
                nc.vector.tensor_scalar(tS, srcf, -1.0, trash[:, 0:1], ALU.mult, ALU.add).then_inc(sem("to_trash"), 1)
                dve.wait_ge(sem("cells"), g + 1)
                nc.vector.tensor_scalar(tC, base, -1.0, trash[:, 1:2], ALU.mult, ALU.add).then_inc(sem("to_trash"), 1)
                dve.wait_ge(sem("to_trash"), 2 * g + 2)
                dve.wait_ge(sem("earlier"), 2 * g + 2)
                nc.vector.scalar_tensor_tensor(tS, preS, 0.0, tS, ALU.is_gt, ALU.mult).then_inc(sem("moved"), 1)
                nc.vector.scalar_tensor_tensor(tC, preP, 0.0, tC, ALU.is_gt, ALU.mult).then_inc(sem("moved"), 1)
                dve.wait_ge(sem("moved"), 2 * g + 2)
                nc.vector.tensor_tensor(sidx[u], tS, srcf, ALU.add).then_inc(sem("index_parts"), 1)
                nc.vector.tensor_tensor(cidx[u], tC, base, ALU.add).then_inc(sem("index_parts"), 1)
                dve.wait_ge(sem("counted"), g + 1)
                dve.wait_ge(sem("index_parts"), 2 * g + 2)
                dve.sem_inc(sem("indexed"), 1)
                if not last:
                    stage(g + 1)
                dve.wait_ge(sem(f"gathered{u}"), 16 * G * (k + 1))
                dve.wait_ge(sem("g_in_psum"), g + 1)
                nc.vector.tensor_tensor(msg.rearrange("p a b -> p (a b)"), gx[u], PS[0:P, 5, :], ALU.mult).then_inc(sem("messages"), 1)

            stage_targets(0, 0)
            stage(0)
            ssp(xT2, XA)
            ssp(Z, XJ)
            ssp(Z, M)
            dve.wait_ge(sem("low_ready"), 1)
            for u in range(2):
                compute(u, u, 0, True, False)
            with dve.Fori(1, NG // 2 - 1) as k:
                for u in range(2):
                    compute(2 * k + u, u, k, False, False)
            for u in range(2):
                compute(NG - 2 + u, u, NG // 2 - 1, False, u == 1)

            nc.vector.memset(AGG[:, HALF - 1, 1, :], 0.0).then_inc(sem("pad_zeroed"), 1)
            dve.wait_ge(sem("sums_loaded0"), 16)
            for u in range(1, ACCS - 1):
                dve.wait_ge(sem(f"sums_loaded{u}"), 16)
                link(nc.vector.tensor_tensor(ACC[0], ACC[0], ACC[u], ALU.add))
            dve.wait_ge(sem(f"sums_loaded{ACCS - 1}"), 16)
            nc.vector.tensor_tensor(AGG[:, :, 0, :], ACC[0][:, 0:HALF, :], ACC[ACCS - 1][:, 0:HALF, :], ALU.add).then_inc(sem("pad_zeroed"), 1)
            nc.vector.tensor_tensor(AGG[:, 0:NT - HALF, 1, :], ACC[0][:, HALF:NT, :], ACC[ACCS - 1][:, HALF:NT, :], ALU.add).then_inc(sem("pad_zeroed"), 1)
            dve.wait_ge(sem("pad_zeroed"), 4)
            dve.sem_inc(sem("sums_ready"), 1)
            dve.wait_ge(sem("sum_blocks"), 1)
            nc.vector.tensor_tensor(M[:, 0:1500].rearrange("p (a b) -> p a b", a=3), M[:, 0:1500].rearrange("p (a b) -> p a b", a=3),
                                    pairs[0], ALU.add).then_inc(sem("m_part"), 1)
            nc.vector.tensor_tensor(M[:, 1500:HC], M[:, 1500:HC], PS[:, 3, 0:P], ALU.add).then_inc(sem("m_part"), 1)
            dve.wait_ge(sem("m_part"), 2)
            dve.sem_inc(sem("m_updated"), 1)
            for k in range(3):
                for a in range(5):
                    dve.wait_ge(sem("product_done"), 10 * k + a + 1)
                    nc.vector.tensor_scalar(cols(Z, a), product(2 * k, a), BC[:, 4 + k:5 + k], None, ALU.add
                                            ).then_inc(sem("block_biased"), 1)
                for a in range(5):
                    dve.wait_ge(sem("block_ln"), 5 * k + a + 1)
                    nc.vector.scalar_tensor_tensor(cols(XA, a), cols(Z, a), 0.0, cols(LG, a), ALU.max, ALU.add).then_inc(sem("block_ssp"), 1)
                for a in range(5):
                    dve.wait_ge(sem("product_done"), 10 * k + 5 + a + 1)
                    nc.vector.scalar_tensor_tensor(cols(M, a), product(2 * k + 1, a), BC[:, 7 + k:8 + k], cols(M, a), ALU.add, ALU.add
                                                   ).then_inc(sem("residual_added"), 1)
            for a in range(5):
                dve.wait_ge(sem("block_ln"), 15 + a + 1)
                nc.vector.scalar_tensor_tensor(cols(XA, a), cols(M, a), 0.0, cols(LG, a), ALU.max, ALU.add).then_inc(sem("block_ssp"), 1)
            for a in range(5):
                dve.wait_ge(sem("product_done"), 30 + a + 1)
                nc.vector.scalar_tensor_tensor(cols(Z, a), cols(xT2, a), BC[:, 3:4], product(6, a), ALU.mult, ALU.add
                                               ).then_inc(sem("gated"), 1)
            for a in range(5):
                dve.wait_ge(sem("gated"), a + 1)
                nc.vector.scalar_tensor_tensor(cols(Z, a), cols(Z, a), BC[:, 2:3], cols(xT2, a), ALU.add, ALU.add
                                               ).then_inc(sem("y_ready"), 1)

            def layernorm(k, dest):
                link(nc.vector.tensor_reduce(lnsum, H, AX, ALU.add))
                link(nc.vector.tensor_scalar(lnsum, lnsum, 1.0 / F, None, ALU.mult))
                nc.vector.tensor_tensor(H, H, lnsum.unsqueeze(2).to_broadcast([P, NT, F]), ALU.subtract).then_inc(sem("ln_centered"), 1)
                dve.wait_ge(sem("ln_squared"), k + 1)
                link(nc.vector.tensor_reduce(lnvar, lnsq, AX, ALU.add))
                nc.vector.tensor_scalar(lnvar, lnvar, 1.0 / F, 1e-5, ALU.mult, ALU.add).then_inc(sem("ln_var"), 1)
                dve.wait_ge(sem("ln_std"), k + 1)
                link(nc.vector.reciprocal(lnvar, lnvar))
                return nc.vector.tensor_tensor(dest, H, lnvar.unsqueeze(2).to_broadcast([P, NT, F]), ALU.mult)

            dve.wait_ge(sem("y_nodes"), 3)
            layernorm(0, X1).then_inc(sem("h_ready"), 1)

            for l in range(2):
                link(nc.vector.memset(hTt[0:F + 1, :], 0.0))
                nc.vector.memset(hTt[F:F + 1, :], 1.0).then_inc(sem("hT_cleared"), 1)
                for h in range(HEADS):
                    nc.vector.memset(V[:, :, h, F:F + 1], 1.0).then_inc(sem("ones_set"), 1)
                for b in range(13):
                    n = min(2, NT - 2 * b)
                    dve.wait_ge(sem("v_in_psum"), 13 * l + b + 1)
                    pv = PS[0:P, 2 + b % 4, 0:n * 192].rearrange("p (t c) -> p t c", t=n)
                    for h in range(HEADS):
                        nc.vector.tensor_copy(V[:, 2 * b:2 * b + n, h, 0:F], pv[:, :, F * h:F * h + F]).then_inc(sem("v_copied"), 1)
                    nc.vector.tensor_copy(SK[:, 2 * b:2 * b + n, :], pv[:, :, 128:192]).then_inc(sem("v_copied"), 1)

                def log_mask(c, i):
                    dve.wait_ge(sem("logged"), c * NT + i + 1)
                    nc.vector.scalar_tensor_tensor(Cb[i % RING], Cb[i % RING], BIG, Lb[i % RING], ALU.mult, ALU.min
                                                   ).then_inc(sem("masked"), 1)

                def score(c, b, i):
                    n = l * ATT + c * NT + i
                    if l == 0:
                        dve.wait_ge(sem("masked"), n + 1)
                    else:
                        dve.wait_ge(sem(f"count_loaded{i % RING}"), 16 * (NT // RING) * c + 16 * (l * ATT // RING + i // RING + 1))
                    dve.wait_ge(sem("scores_in_psum"), n + 1)
                    nc.vector.tensor_tensor(Tt[:, b, i], score_ring[i % BANKS].rearrange("p (h d) -> p h d", h=HEADS),
                                            Cb[i % RING].unsqueeze(1).to_broadcast([P, HEADS, D]), ALU.add).then_inc(sem("scored"), 1)

                def running(c, b, i):
                    n = l * ATT + c * NT + i
                    dve.wait_ge(sem("scored"), n + 1)
                    if i == 0:
                        nc.vector.tensor_copy(RM, Tt[:, b, 0]).then_inc(sem("max_run"), 1)
                    else:
                        dve.wait_ge(sem("max_run"), n)
                        nc.vector.tensor_tensor(RM, RM, Tt[:, b, i], ALU.max).then_inc(sem("max_run"), 1)

                def column_max(c):
                    dve.wait_ge(sem("max_moved"), l * NC + c + 1)
                    nc.vector.tensor_reduce(mrow, PS[0:P, 7, 0:HEADS * D].rearrange("p (a b) -> p a b", b=P), AX, ALU.max
                                            ).then_inc(sem("max_reduced"), 1)
                    dve.wait_ge(sem("max_reduced"), l * NC + c + 1)
                    nc.vector.tensor_scalar(mrow, mrow, FLOOR, None, ALU.max).then_inc(sem("max_ready"), 1)

                def stage_att(c, b, first):
                    for i in range(NT + 2):
                        if i < NT and l == 0:
                            log_mask(c, i)
                        if i >= 2:
                            score(c, b, i - 2)
                            if i == 2 and not first:
                                column_max(c - 1)
                            running(c, b, i - 2)

                stage_att(0, 0, True)
                with dve.Fori(0, NC // 2) as k:
                    stage_att(2 * k + 1, 1, False)
                    stage_att(2 * k + 2, 0, False)
                column_max(NC - 1)

                dve.wait_ge(sem("att_copied"), 9 * (l + 1))
                link(nc.vector.tensor_scalar(rec, NDn[:, :, :, F], 1e-16, None, ALU.add))
                link(nc.vector.reciprocal(rec, rec))
                link(nc.vector.tensor_tensor(att, NDn.rearrange("p t h c -> p (t h) c")[:, :, 0:F],
                                             rec.rearrange("p t h -> p (t h)").unsqueeze(2).to_broadcast([P, NT * HEADS, F]), ALU.mult))
                link(nc.vector.tensor_tensor(H, att4[:, :, 0, :], att4[:, :, 1, :], ALU.add))
                ins = nc.vector.scalar_tensor_tensor(H, H, 0.5, SK, ALU.mult, ALU.add)
                if l == 0:
                    link(ins)
                    dve.sem_inc(sem("h_ready"), 1)
                else:
                    link(ins)
            link(nc.vector.tensor_tensor(H, H, X1, ALU.add))
            layernorm(1, H).then_inc(sem("result_ready"), 1)

        @block.tensor
        def _(pe):
            lin_n = [0]

            def lin(w, v):
                pe.wait_ge(sem("lin_used"), lin_n[0])
                lin_n[0] += 1
                for a in range(5):
                    ins = nc.tensor.matmul(PS[:, a, 0:LC], BD[:, w, :], v[:, a * LC:(a + 1) * LC], start=True, stop=True)
                ins.then_inc(sem("lin_done"), 1)

            pe.wait_ge(sem("ident_ready"), 1)
            pe.wait_ge(sem("x_loaded"), 32)
            pe.wait_ge(sem("pad_zeroed"), 1)

            def to_features(a, name):
                for j in range(HALF):
                    ins = nc.tensor.transpose(block_at[j], a[:, j, :, :].rearrange("p h f -> p (h f)"), ident[0:P, 0:P])
                ins.then_inc(sem(name), 1)

            def to_nodes(a, name):
                for j in range(HALF):
                    ins = nc.tensor.transpose(node_at[j], a[:, j * P:(j + 1) * P], ident[:, :])
                ins.then_inc(sem(name), 1)

            to_features(X, "x_blocks")
            pe.wait_ge(sem("weights_loaded"), 16 * 22)
            for i in range(9):
                ins = nc.tensor.transpose(PS[:, 4 + i // 4, (i % 4) * 128:(i % 4 + 1) * 128], BDraw[:, i, :], ident[:, :])
            ins.then_inc(sem("bd_in_psum"), 1)
            pe.wait_ge(sem("watt_loaded"), 16)
            nc.tensor.transpose(PS[0:R, 7, 0:F], Watt, ident[0:F, 0:F]).then_inc(sem("watt_in_psum"), 1)
            pe.wait_ge(sem("bd_ready"), 2)
            pe.wait_ge(sem("ssp_done"), 1)
            lin(1, XA)
            pe.wait_ge(sem("ssp_done"), 2)
            to_nodes(XJ, "xj_in_psum")
            pe.wait_ge(sem("xj_part"), 4)
            lin(0, XA)

            pe.wait_ge(sem("lin_used"), 2)
            pe.wait_ge(sem("ident16_ready"), 1)
            pe.wait_ge(sem("wattT_copied"), 1)

            def edge_group(g, u, k):
                pe.wait_ge(sem("staged"), g + 1)
                pe.wait_ge(sem("matched"), 4 * g)
                for key, bank in ((srch, 0), (dsth, 2)):
                    for s in range(G):
                        ins = nc.tensor.matmul(PS[0:P, bank + s // 4, (s % 4) * P:(s % 4 + 1) * P],
                                               key[:, s:s + 1].to_broadcast([P, P]), identh[0:P, 0:P], start=True, stop=True)
                ins.then_inc(sem("keys_in_psum"), 1)
                pe.wait_ge(sem(f"f_loaded{u}"), 16 * (k + 1))
                pe.wait_ge(sem("fT_copied"), g)
                nc.tensor.transpose(PS[:, 4, 0:P], f8[u], ident[0:P, 0:P]).then_inc(sem("fT_in_psum"), 1)
                pe.wait_ge(sem("fT_copied"), g + 1)
                pe.wait_ge(sem("messages"), g)
                nc.tensor.matmul(PS[0:P, 5, :], fT, Wblk, start=True, stop=True).then_inc(sem("g_in_psum"), 1)
                pe.wait_ge(sem("matched"), 4 * g + 4)
                pe.wait_ge(sem("messages"), g + 1)
                pe.wait_ge(sem("combined"), g)
                for s in range(G):
                    ins = nc.tensor.matmul(PS[0:P, 6, s * F:(s + 1) * F], SelS[:, s, :], msg[:, s, :], start=True, stop=True)
                ins.then_inc(sem("comb_in_psum"), 1)

            pe.wait_ge(sem("wblk_ready"), 16 * G)
            for u in range(2):
                edge_group(u, u, 0)
            with pe.Fori(1, NG // 2) as k:
                for u in range(2):
                    edge_group(2 * k + u, u, k)

            pe.wait_ge(sem("sums_ready"), 1)
            to_features(AGG, "sum_blocks")
            pe.wait_ge(sem("m_updated"), 1)
            for k in range(3):
                for a in range(5):
                    if k:
                        pe.wait_ge(sem("residual_added"), 5 * (k - 1) + a + 1)
                    nc.tensor.matmul(product(2 * k, a), BD[:, 3 + k, :], cols(M, a), start=True, stop=True).then_inc(sem("product_done"), 1)
                for a in range(5):
                    pe.wait_ge(sem("block_ssp"), 5 * k + a + 1)
                    nc.tensor.matmul(product(2 * k + 1, a), BD[:, 6 + k, :], cols(XA, a), start=True, stop=True).then_inc(sem("product_done"), 1)
            for a in range(5):
                pe.wait_ge(sem("block_ssp"), 15 + a + 1)
                nc.tensor.matmul(product(6, a), BD[:, 2, :], cols(XA, a), start=True, stop=True).then_inc(sem("product_done"), 1)
            pe.wait_ge(sem("y_ready"), 5)
            to_nodes(Z, "y_in_psum")

            pe.wait_ge(sem("layer_weights"), 16 * 16)
            for l in range(2):
                Hin = X1 if l == 0 else H
                pe.wait_ge(sem("h_ready"), l + 1)
                for b in range(7):
                    n = min(4, NT - 4 * b)
                    for t in range(n):
                        ins = nc.tensor.transpose(PS[0:F, b, t * P:(t + 1) * P], Hin[:, 4 * b + t, :], ident[0:P, 0:P])
                    ins.then_inc(sem("h_block"), 1)
                pe.wait_ge(sem("hT_copied"), 7 * (l + 1))

                def qk(c, w, bank, n):
                    pe.wait_ge(sem("qk_copied"), max(n - 1, 0))
                    nc.tensor.matmul(PS[:, bank, 0:QC], w, hT[:, c * QC:(c + 1) * QC], start=True, stop=True).then_inc(sem("qk_in_psum"), 1)

                def values(b):
                    n = min(2, NT - 2 * b)
                    v = 13 * l + b
                    pe.wait_ge(sem("v_copied"), 3 * max(v - 3, 0))
                    for t in range(n):
                        ins = nc.tensor.matmul(PS[0:P, 2 + b % 4, t * 192:(t + 1) * 192], hT[:, (2 * b + t) * P:(2 * b + t + 1) * P], wv_(l), start=True, stop=True)
                    ins.then_inc(sem("v_in_psum"), 1)

                for c in range(10):
                    qk(c, wq_(l), 0, 20 * l + 2 * c)
                    qk(c, wk_(l), 1, 20 * l + 2 * c + 1)
                    values(c)
                for b in range(10, 13):
                    values(b)
                pe.wait_ge(sem("qk_copied"), 20 * (l + 1))
                pe.wait_ge(sem("v_copied"), 39 * (l + 1))
                pe.wait_ge(sem("ones_set"), 2 * (l + 1))

                def scores(c, i):
                    n = l * ATT + c * NT + i
                    if not (isinstance(n, int) and n < BANKS):
                        pe.wait_ge(sem("scored"), n if i == 0 else n - BANKS + 1)
                    nc.tensor.matmul(score_ring[i % BANKS], kT[:, i * P:(i + 1) * P], qc, start=True, stop=True
                                     ).then_inc(sem("scores_in_psum"), 1)

                def weighted(c, b, i):
                    n = l * ATT + c * NT + i
                    pe.wait_ge(sem("weighed"), n + 1)
                    if i == 0:
                        pe.wait_ge(sem("attended"), 2 * (l * NC + c + 1))
                    for h in range(HEADS):
                        ins = nc.tensor.matmul(PS[0:VW, 6, h * D:(h + 1) * D], V[:, i, h, :], Tt[:, b, i, h, :],
                                               start=i == 0 and h == 0, stop=i == NT - 1, skip_group_check=True)
                    ins.then_inc(sem("weighted_sums"), 1)

                def move_max(c):
                    pe.wait_ge(sem("max_run"), l * ATT + (c + 1) * NT)
                    for q in range(BLK * HEADS):
                        ins = nc.tensor.transpose(PS[0:P, 7, q * P:(q + 1) * P], Rt[0:P, q * P:(q + 1) * P], ident[0:P, 0:P])
                    ins.then_inc(sem("max_moved"), 1)

                def spread_max(c):
                    pe.wait_ge(sem("max_ready"), l * NC + c + 1)
                    for q in range(BLK * HEADS):
                        ins = nc.tensor.matmul(PS[0:P, 7, q * P:(q + 1) * P], mrow[:, q:q + 1].to_broadcast([P, P]),
                                               ident[0:P, 0:P], start=True, stop=True)
                    ins.then_inc(sem("max_in_psum"), 1)

                def stage_att(c, b, first, last):
                    if not last:
                        pe.wait_ge(sem("qc_ready"), HEADS * (l * NC + c + 1))
                    for i in range(LAG):
                        if not last:
                            scores(c, i)
                        if not first and i == 0:
                            move_max(c - 1)
                        if not first and i == LAG - 1:
                            spread_max(c - 1)
                    for i in range(NT):
                        if not last and i + LAG < NT:
                            scores(c, i + LAG)
                        if not first:
                            weighted(c - 1, 1 - b, i)

                stage_att(0, 0, True, False)
                with pe.Fori(0, NC // 2) as k:
                    stage_att(2 * k + 1, 1, False, False)
                    stage_att(2 * k + 2, 0, False, False)
                stage_att(NC, 1, False, True)
                pe.wait_ge(sem("attended"), 2 * (NC * (l + 1) + 1))
                for b in range(9):
                    n = min(3, NT - 3 * b)
                    if b >= 6:
                        pe.wait_ge(sem("att_copied"), 9 * l + b - 5)
                    for t in range(3 * b, 3 * b + n):
                        for h in range(HEADS):
                            o = (2 * (t - 3 * b) + h) * VW
                            ins = nc.tensor.transpose(PS[0:P, b % 6, o:o + VW], AO[h][:, t * P:(t + 1) * P], ident[0:VW, 0:VW])
                    ins.then_inc(sem("att_block"), 1)



_INS = ['x', 'src', 'dst', 'edge_attr_16', 'L0_gnn_W_att', 'L0_gnn_W_i', 'L0_gnn_b_i', 'L0_gnn_W_j', 'L0_gnn_b_j', 'L0_gnn_W_v', 'L0_gnn_b_v', 'L0_gnn_res_dense_W', 'L0_gnn_res_dense_b', 'L0_gnn_res_res_W', 'L0_gnn_res_res_b', 'L0_gnn_gate', 'L1_gnn_l1_wq', 'L1_gnn_l1_bq', 'L1_gnn_l1_wk', 'L1_gnn_l1_bk', 'L1_gnn_l1_wv', 'L1_gnn_l1_bv', 'L1_gnn_l1_ws', 'L1_gnn_l1_bs', 'L1_gnn_l2_wq', 'L1_gnn_l2_bq', 'L1_gnn_l2_wk', 'L1_gnn_l2_bk', 'L1_gnn_l2_wv', 'L1_gnn_l2_bv', 'L1_gnn_l2_ws', 'L1_gnn_l2_bs']
_OUTS = [((3125, 64), 'float32')]


def kernel(**inputs):
    import numpy as _np
    import concourse.bacc as _bacc
    from concourse import mybir as _mybir
    from concourse.bass_utils import run_bass_kernel_spmd as _run

    nc = _bacc.Bacc("TRN2", target_bir_lowering=False, num_devices=1)
    arrays, args = {}, []
    for name in _INS:
        a = _np.ascontiguousarray(inputs[name])
        arrays[f"in_{name}_dram"] = a
        args.append(nc.dram_tensor(f"in_{name}_dram", a.shape, _mybir.dt.from_np(a.dtype), kind="ExternalInput").ap())
    for i, (shape, dtype) in enumerate(_OUTS):
        dt = _mybir.dt.from_np(_np.dtype(dtype))
        args.append(nc.dram_tensor(f"out_{i}_dram", shape, dt, kind="ExternalOutput").ap())
    build(nc, *args)
    r = _run(nc, [arrays], core_ids=[0])
    return r.results[0]["out_0_dram"]
```

```python
from contextlib import ExitStack

import concourse.bass as bass
from concourse import mybir

N = 3125
E = 100000
F = 64
R = 16
P = 125
NT = N // P
G = 8
EP = 128
EJ = -(-E // (EP * 2 * G)) * 2 * G
NG = EJ // G
LASTP = E - (EP - 1) * EJ
LASTG = LASTP // G
assert 0 < LASTP and LASTP % (2 * G) == 0 and 2 * LASTG >= NG
HALF = (NT + 1) // 2
HC = HALF * P
LC = HC // 5
NC = 13
BLK = 2
MW = -(-N // (NC * BLK))
D = BLK * MW
ND = NC * D
QKN = 11
QC = ND // QKN
assert MW <= P and 2 * D <= 512 and QC * QKN == ND and QC <= 512
FILLS = 25
FILL = -(-(N * ND + EP) // (128 * FILLS))
RING = 5
BANKS = 6
LAG = 5
LOG_LAG = 3
ACCS = 2
TURNS = G // ACCS
BIG = 1e30
FLOOR = -1e20
HEADS = 2
EXP_LN_SET = 6
VW = F + 1
ATT = NC * NT


def build(nc, x, src, dst, edge_attr, W_att, W_i, b_i, W_j, b_j, W_v, b_v, rd_W, rd_b, rr_W, rr_b, gate,
          wq1, bq1, wk1, bk1, wv1, bv1, ws1, bs1, wq2, bq2, wk2, bk2, wv2, bv2, ws2, bs2, out):
    f32 = mybir.dt.float32
    f16 = mybir.dt.float16
    i32 = mybir.dt.int32
    ALU = mybir.AluOpType
    ACT = mybir.ActivationFunctionType
    AX = mybir.AxisListType.X
    layers = [(wq1, bq1, wk1, bk1, wv1, bv1, ws1, bs1), (wq2, bq2, wk2, bk2, wv2, bv2, ws2, bs2)]

    xj_dram = nc.dram_tensor("xj_rows", [N, F], f32, kind="Internal").ap()
    acc_dram = [nc.dram_tensor(f"message_sums{u}", [N + EP, F], f32, kind="Internal").ap() for u in range(ACCS)]
    cnt_dram = nc.dram_tensor("edge_counts", [128 * FILLS * FILL, 1], f32, kind="Internal").ap()
    cnt_fills = cnt_dram.rearrange("(p a b) o -> p a (b o)", p=128, a=FILLS)
    cnt_rows = cnt_dram[0:N * ND, :].rearrange("(t p d) o -> p t (d o)", p=P, t=NT)
    log_dram = nc.dram_tensor("log_counts", [NT, P, ND], f32, kind="Internal").ap()

    ctx = ExitStack()
    with ctx:
        ctx.enter_context(nc.allow_non_contiguous_dma(reason="short bias columns"))

        def sb(name, cols, dt=f32):
            return ctx.enter_context(nc.sbuf_tensor(name, [128, cols], dt))

        sems = {}

        def sem(name):
            if name not in sems:
                sems[name] = ctx.enter_context(nc.semaphore(name))
            return sems[name]

        T = sb("scores", 2 * NT * HEADS * D)
        Xt = sb("x_nodes", (NT + 1) * F)
        X1t = sb("x1_nodes", NT * F)
        Ht = sb("h_nodes", NT * F)
        SKt = sb("skip_nodes", NT * F)
        hTt = sb("h_features", ND)
        qTt = sb("q_features", ND)
        kTt = sb("k_features", ND)
        Vt = sb("v_nodes", NT * HEADS * VW)
        O1t = sb("attended1", ND)
        Rt = sb("running_max", HEADS * D)
        MBt = sb("max_of_targets", HEADS * D)
        CL = sb("counts_and_logs", 2 * RING * D)
        qct = sb("q_chunk", HEADS * D)
        WL = sb("layer_weights", 2 * (128 + 128 + 192))
        BC = sb("bias_columns", 12)
        ident = sb("identity", 128)
        identh = sb("identity16", 128, f16)
        small = sb("small", 192)
        halfc = sb("half_column", 1)
        kh = sb("keys16", 2 * G, f16)
        PS = ctx.enter_context(nc.psum_tensor("PS", [128, 8, 512], f32))

        def grid(t, a, off=0, b=None, parts=128):
            return t[0:parts, off:off + a * b].rearrange("p (a b) -> p a b", b=b)

        X = Xt[0:P, :].rearrange("p (j h f) -> p j h f", h=2, f=F)
        X1 = grid(X1t, NT, 0, F, P)
        H = grid(Ht, NT, 0, F, P)
        SK = grid(SKt, NT, 0, F, P)
        BD = grid(SKt, 9, 0, 128)
        BDraw = grid(T, 9, 0, 128)
        xT2 = O1t[:, 0:HC]
        M = kTt[:, 0:HC]
        Z = qTt[:, 0:HC]
        LG = Vt[:, 0:HC]
        XA = hTt[:, 0:HC]
        XJ = T[:, 1200:1200 + HC]
        XJn = grid(T, NT + 1, 3000, F, P)
        zero_tile = T[0:P, 5000:5000 + 26 * F]
        cfill = T[:, 21000:21000 + FILL]

        at = [7000]

        def take(n):
            at[0] += n
            return at[0] - n

        o = take(EJ)
        src_i = T[:, o:o + EJ].bitcast(i32)
        dst_o = o = take(EJ)
        dst_i = T[:, o:o + EJ].bitcast(i32)
        SelS = grid(T, G, take(G * EP), EP)
        SelD = grid(T, G, take(G * EP), EP)
        SelP = grid(T, G, take(G * EP), EP)
        tmpP = grid(T, G, take(G * EP), EP)
        tmpS = grid(T, G, take(G * EP), EP)
        gx = [T[:, o:o + G * F] for o in (take(G * F), take(G * F))]
        msg = grid(T, G, take(G * F), F)
        cm = [T[:, o:o + G * F] for o in (take(G * F), take(G * F))]
        f8 = [T[:, o:o + G * R] for o in (take(G * R), take(G * R))]
        o = take(EP)
        fT = T[:, o:o + EP]
        o = take(G * F)
        Wblk = T[:, o:o + G * F]
        o = take(EP)
        low = T[:, o:o + EP]
        o = take(R)
        Watt = T[0:F, o:o + R]
        o = take(F)
        WattT = T[0:R, o:o + F]
        assert at[0] <= 21000
        sc = [0]

        def col(n):
            sc[0] += n
            assert sc[0] <= 160
            return small[:, sc[0] - n:sc[0]]

        srcf, dstf, tS, tC, base, preS, preP = (col(G) for _ in range(7))
        dcur = [col(G).bitcast(i32) for _ in range(2)]
        sidx = [col(G).bitcast(i32) for _ in range(2)]
        cidx = [col(G).bitcast(i32) for _ in range(2)]
        cnt = [col(G) for _ in range(2)]
        trash_i = col(2).bitcast(i32)
        trash = col(2)
        srch, dsth = kh[:, 0:G], kh[:, G:2 * G]

        ACC = [grid(T, NT, u * NT * F, F, P) for u in range(ACCS)]
        AGG = X

        Tt = T[0:P, :].rearrange("p (b i h d) -> p b i h d", b=2, i=NT, h=HEADS)
        RM = Rt[0:P, :].rearrange("p (h d) -> p h d", h=HEADS)
        MB = MBt[0:P, :].rearrange("p (h d) -> p h d", h=HEADS)
        Cb = [CL[0:P, r * D:(r + 1) * D] for r in range(RING)]
        Lb = [CL[0:P, (RING + r) * D:(RING + r + 1) * D] for r in range(RING)]
        hT = hTt[:, :]
        qT, kT, qc = qTt[:, :], kTt[:, :], qct[:, :]
        V = Vt[0:P, :].rearrange("p (t h c) -> p t h c", t=NT, h=HEADS)
        AO = [hTt[0:VW, :], O1t[0:VW, :]]
        mrow = small[0:MW, 160:160 + BLK * HEADS]
        NDn = T[0:P, 0:NT * HEADS * VW].rearrange("p (t h c) -> p t h c", t=NT, h=HEADS)
        rec = T[0:P, 4000:4000 + NT * HEADS].rearrange("p (t h) -> p t h", t=NT)
        att = grid(T, NT * HEADS, 5000, F, P)
        att4 = T[0:P, 5000:5000 + NT * HEADS * F].rearrange("p (t h c) -> p t h c", t=NT, h=HEADS)
        lnsum, lnvar = T[0:P, 9000:9000 + NT], T[0:P, 9100:9100 + NT]
        lnsq = grid(T, NT, 10000, F, P)

        def wq_(l):
            return WL[:, l * 448:l * 448 + 128]

        def wk_(l):
            return WL[:, l * 448 + 128:l * 448 + 256]

        def wv_(l):
            return WL[:, l * 448 + 256:l * 448 + 448]

        pairs = [PS[:, 0:3, 0:500], PS[:, 3:4, 0:P]]
        block_at = [PS[:, j // 4, (j % 4) * P:(j % 4 + 1) * P] for j in range(HALF)]
        node_at = [PS[0:P, j // 4, (j % 4) * 128:(j % 4 + 1) * 128] for j in range(HALF)]
        score_ring = [PS[0:P, r, 0:HEADS * D] for r in range(BANKS)]
        lin5 = PS[:, 0:5, 0:LC]

        def qk_bank(n):
            return PS[:, n % BANKS, 0:QC]

        def product(stage, a):
            return PS[:, (5 * stage + a) % 8, 0:LC]

        def cols(v, a):
            return v[:, a * LC:(a + 1) * LC]


        def five(v):
            return v.rearrange("p (a b) -> p a b", a=5)

        def edge_parts(a):
            return [(slice(0, EP - 1), a[0:(EP - 1) * EJ]), (slice(EP - 1, EP), a[(EP - 1) * EJ:E])]

        def load_features(eng, g, u, last):
            for (q, rows), first in zip(edge_parts(edge_attr), (g, g - LASTG if last else g)):
                v = rows.rearrange("(p j) r -> p (j r)", p=q.stop - q.start)
                eng.dma_start(f8[u][q, :], v[:, bass.ds(first * (G * R), G * R)]).then_inc(sem(f"f_loaded{u}"), 16)

        block = ctx.enter_context(nc.Block())

        @block.sync
        def _(sp):
            xv = x.rearrange("(t p) f -> p t f", p=P)
            sp.dma_start(X[:, :, 0, :], xv[:, 0:HALF, :]).then_inc(sem("x_loaded"), 16)
            sp.dma_start(X[:, 0:NT - HALF, 1, :], xv[:, HALF:NT, :]).then_inc(sem("x_loaded"), 16)
            sp.wait_ge(sem("bd_zeroed"), 1)
            for h in range(2):
                q = slice(64 * h, 64 * h + 64)
                for i, w in enumerate((W_i, W_j, W_v)):
                    sp.dma_start(BDraw[q, i, q], w).then_inc(sem("weights_loaded"), 16)
                for i, w in ((3, rd_W), (6, rr_W)):
                    sp.dma_start(BDraw[q, i:i + 3, q], w.rearrange("k g f -> g k f")).then_inc(sem("weights_loaded"), 16)
                for i, b in enumerate((b_i, b_j, b_v, gate)):
                    sp.dma_start(BC[q, i:i + 1], b.rearrange("(f o) -> f o", o=1)).then_inc(sem("weights_loaded"), 16)
                for i, b in ((4, rd_b), (7, rr_b)):
                    sp.dma_start(BC[q, i:i + 3], b.rearrange("k f -> f k")).then_inc(sem("weights_loaded"), 16)
            sp.dma_start(Watt, W_att).then_inc(sem("watt_loaded"), 16)
            sp.wait_ge(sem("edges_padded"), 2)
            for a, dest in ((src, src_i), (dst, dst_i)):
                for q, keys in edge_parts(a):
                    sp.dma_start(dest[q, 0:EJ if q.start == 0 else LASTP], keys.rearrange("(p j) -> p j", p=q.stop - q.start)
                                 ).then_inc(sem("edges_loaded"), 16)
            sp.wait_ge(sem("fills_set"), 2)
            for u in range(ACCS):
                sp.dma_start(acc_dram[u][0:N + P, :].rearrange("(p t) f -> p (t f)", p=P), zero_tile).then_inc(sem("sums_cleared"), 16)
                sp.dma_start(acc_dram[u][N + P:N + EP, :], zero_tile[0:EP - P, 0:F]).then_inc(sem("sums_cleared"), 16)
            for a in range(3, FILLS):
                if a == 5:
                    sp.wait_ge(sem("xj_stored"), 16)
                    for u in range(2):
                        sp.wait_ge(sem(f"f_loaded{u}"), 32)
                sp.dma_start(cnt_fills[:, a, :], cfill).then_inc(sem("counts_cleared"), 16)
            sp.wait_ge(sem("weights_cleared"), 1)
            for l, (wq, bq, wk, bk, wv, bv, ws, bs) in enumerate(layers):
                for w, b, dest in ((wq, bq, wq_(l)), (wk, bk, wk_(l)), (wv, bv, wv_(l)[:, 0:128]), (ws, bs, wv_(l)[:, 128:192])):
                    sp.dma_start(dest[0:F, :], w).then_inc(sem("layer_weights"), 16)
                    sp.dma_start(dest[F:F + 1, :], b.rearrange("(o f) -> o f", o=1)).then_inc(sem("layer_weights"), 16)
            def load_f(g, u, last):
                sp.wait_ge(sem("fT_in_psum"), g - 1)
                load_features(sp, g, u, last)

            for first, end, last in ((1, LASTG // 2, False), (LASTG // 2, NG // 2, True)):
                with sp.Fori(first, end) as k:
                    for u in range(2):
                        load_f(2 * k + u, u, last)

            for u in range(ACCS):
                sp.wait_ge(sem(f"sum_added{u}"), 16 * TURNS * NG)
                sp.dma_start(ACC[u], acc_dram[u][0:N, :].rearrange("(t p) f -> p t f", p=P)).then_inc(sem(f"sums_loaded{u}"), 16)

            sp.wait_ge(sem("count_added"), 16 * EJ)
            for l in range(2):
                if l:
                    for r in range(RING):
                        sp.wait_ge(sem(f"log_stored{r}"), 16 * ATT // RING)

                def settled():
                    sp.sem_inc(sem("sync_waited"), 1)

                def load(c, i):
                    n = l * ATT + c * NT + i
                    r = i % RING
                    if not (isinstance(n, int) and n < RING):
                        sp.wait_ge(sem("scored"), n - RING + 1)
                        settled()
                        if l == 0:
                            sp.wait_ge(sem(f"log_stored{r}"), 16 * (NT // RING) * c + 16 * (i // RING))
                        settled()
                    src_rows = log_dram.rearrange("t p d -> p t d") if l else cnt_rows
                    sp.dma_start(Cb[r], src_rows[:, i, bass.ds(c * D, D)]).then_inc(sem(f"count_loaded{r}"), 16)

                def store(c, i):
                    n = l * ATT + c * NT + i
                    sp.wait_ge(sem("masked"), n + 1)
                    settled()
                    sp.dma_start(log_dram[i, :, bass.ds(c * D, D)], Cb[i % RING]).then_inc(sem(f"log_stored{i % RING}"), 16)

                def chunk(c):
                    for i in range(NT + 3):
                        if i < NT:
                            load(c, i)
                        if l == 0 and i >= 3:
                            store(c, i - 3)

                chunk(0)
                with sp.Fori(1, NC) as c:
                    chunk(c)
            sp.wait_ge(sem("result_ready"), 1)
            sp.dma_start(out.rearrange("(t p) f -> p t f", p=P), H).then_inc(sem("stored"), 16)
            sp.wait_ge(sem("stored"), 16)

        @block.gpsimd
        def _(pool):
            nc.gpsimd.memset(BDraw, 0.0).then_inc(sem("bd_zeroed"), 1)
            nc.gpsimd.memset(ident[:, :], 0.0).then_inc(sem("ident_zeroed"), 1)
            pool.wait_ge(sem("ident_zeroed"), 1)
            nc.gpsimd.affine_select(out=ident[:, :], in_=ident[:, :], compare_op=ALU.not_equal, fill=1.0, base=0,
                                    pattern=[[-1, 128]], channel_multiplier=1).then_inc(sem("ident_ready"), 1)
            nc.gpsimd.iota(src_i[:, LASTP:EJ], pattern=[[0, EJ - LASTP]], base=N, channel_multiplier=0).then_inc(sem("edges_padded"), 1)
            nc.gpsimd.memset(T[:, dst_o + LASTP:dst_o + EJ], 0.0).then_inc(sem("edges_padded"), 1)
            nc.gpsimd.memset(zero_tile, 0.0).then_inc(sem("fills_set"), 1)
            nc.gpsimd.memset(cfill, -0.5).then_inc(sem("fills_set"), 1)
            nc.gpsimd.memset(WL[:, :], 0.0).then_inc(sem("weights_cleared"), 1)
            nc.gpsimd.memset(Wblk, 0.0).then_inc(sem("wblk_zeroed"), 1)
            nc.gpsimd.memset(low, 1.0).then_inc(sem("low_set"), 1)
            pool.wait_ge(sem("low_set"), 1)
            nc.gpsimd.affine_select(out=low, in_=low, compare_op=ALU.is_gt, fill=0.0, base=0,
                                    pattern=[[-1, EP]], channel_multiplier=1).then_inc(sem("low_ready"), 1)
            nc.gpsimd.iota(trash_i[:, 0:1], pattern=[[0, 1]], base=N, channel_multiplier=1).then_inc(sem("trash_iota"), 1)
            nc.gpsimd.iota(trash_i[:, 1:2], pattern=[[0, 1]], base=N * ND, channel_multiplier=1).then_inc(sem("trash_iota"), 1)

            def settled():
                pool.sem_inc(sem("pool_waited"), 1)

            def gather(g, u, s):
                pool.indirect_dma_start(gx[u][:, s * F:(s + 1) * F], None, xj_dram,
                                        bass.IndirectOffsetOnAxis(ap=dcur[u][:, s:s + 1], axis=0)
                                        ).then_inc(sem(f"gathered{u}"), 16)

            def scatter(g, u, s):
                a = s % ACCS
                pool.wait_ge(sem(f"sum_added{a}"), 16 * (TURNS * g + s // ACCS))
                settled()
                pool.indirect_dma_start(acc_dram[a], bass.IndirectOffsetOnAxis(ap=sidx[u][:, s:s + 1], axis=0),
                                        cm[u][:, s * F:(s + 1) * F], None, compute_op=ALU.add
                                        ).then_inc(sem(f"sum_added{a}"), 16)
                pool.wait_ge(sem("count_added"), 16 * G * g + 16 * s)
                settled()
                pool.indirect_dma_start(cnt_dram, bass.IndirectOffsetOnAxis(ap=cidx[u][:, s:s + 1], axis=0),
                                        cnt[u][:, s:s + 1], None, compute_op=ALU.add
                                        ).then_inc(sem("count_added"), 16)

            def group(g, u, gathers, scatters):
                if gathers:
                    pool.wait_ge(sem("targets_staged"), g + 1)
                if scatters:
                    pool.wait_ge(sem("combined"), g - 1)
                    pool.wait_ge(sem("indexed"), g - 1)
                settled()
                for s in range(G):
                    if gathers:
                        gather(g, u, s)
                    if scatters:
                        scatter(g - 2, u, s)

            pool.wait_ge(sem("xj_stored"), 16)
            for u in range(2):
                group(u, u, True, False)
            pool.wait_ge(sem("sums_cleared"), 32 * ACCS)
            pool.wait_ge(sem("counts_cleared"), 16 * FILLS)
            for u in range(2):
                group(2 + u, u, True, True)
            with pool.Fori(2, NG // 2) as k:
                for u in range(2):
                    group(2 * k + u, u, True, True)
            for u in range(2):
                group(NG + u, u, False, True)

            for l in range(2):
                if l == 0:
                    pool.wait_ge(sem("y_ready"), 5)
                    nc.gpsimd.memset(hTt[F:128, :], 0.0).then_inc(sem("hT_zeroed"), 1)
                    pool.wait_ge(sem("hT_zeroed"), 1)
                else:
                    pool.wait_ge(sem("att_block"), 9 * l)
                nc.gpsimd.memset(hTt[F:F + 1, :], 1.0).then_inc(sem("hT_cleared"), 1)

                def shift(c, b, i):
                    if i == 0:
                        pool.wait_ge(sem("max_spread"), l * NC + c + 1)
                    nc.gpsimd.tensor_tensor(Tt[:, b, i], Tt[:, b, i], MB, ALU.subtract).then_inc(sem("shifted"), 1)

                with pool.Fori(0, NC // 2) as k:
                    for b in range(2):
                        for i in range(NT):
                            shift(2 * k + b, b, i)
                for i in range(0, NT, 2):
                    shift(NC - 1, 0, i)

        @block.scalar
        def _(act):
            ssp_n, lin_n = [0], [0]

            def load_exp_ln():
                act.add_instruction(mybir.InstLoadActFuncSet(name=nc.get_next_instruction_name(), engine=mybir.EngineType.Activation, act_func_set_id=EXP_LN_SET, ins=[], outs=[]))

            load_exp_ln()

            act.wait_ge(sem("fills_set"), 2)
            for a in range(3):
                act.dma_start(cnt_fills[:, a, :], cfill).then_inc(sem("counts_cleared"), 16)

            def ssp(z):
                k = ssp_n[0]
                ssp_n[0] += 1
                act.wait_ge(sem("ssp_done"), k)
                nc.scalar.activation(LG, z, ACT.Abs).then_inc(sem("ssp_abs"), 1)
                act.wait_ge(sem("ssp_abs"), k + 1)
                nc.scalar.activation(LG, LG, ACT.Exp, scale=-1.0).then_inc(sem("ssp_exp"), 1)
                act.wait_ge(sem("ssp_exp"), k + 1)
                nc.scalar.activation(LG, LG, ACT.Ln, scale=0.5, bias=halfc[:, :]).then_inc(sem("ssp_ln"), 1)

            def lin_bias(b):
                lin_n[0] += 1
                act.wait_ge(sem("lin_done"), lin_n[0])
                act.wait_ge(sem("ssp_done"), ssp_n[0])
                nc.scalar.activation(five(Z), lin5, ACT.Identity, bias=BC[:, b:b + 1]).then_inc(sem("lin_used"), 1)
                act.wait_ge(sem("lin_used"), lin_n[0])

            act.wait_ge(sem("x_blocks"), 1)
            nc.scalar.activation(xT2[:, 0:1500].rearrange("p (a b) -> p a b", a=3), pairs[0], ACT.Copy).then_inc(sem("xT_copied"), 1)
            nc.scalar.activation(xT2[:, 1500:HC].rearrange("p (a b) -> p a b", a=1), pairs[1], ACT.Copy).then_inc(sem("xT_copied"), 1)
            act.wait_ge(sem("xT_copied"), 2)
            act.wait_ge(sem("half_set"), 1)
            ssp(xT2)
            act.wait_ge(sem("bd_in_psum"), 1)
            nc.scalar.activation(BD[:, 0:8, :].rearrange("p (a b) c -> p a (b c)", a=2), PS[:, 4:6, :], ACT.Copy).then_inc(sem("bd_ready"), 1)
            nc.scalar.activation(BD[:, 8, :], PS[:, 6, 0:128], ACT.Copy).then_inc(sem("bd_ready"), 1)
            act.wait_ge(sem("watt_in_psum"), 1)
            nc.scalar.activation(WattT, PS[0:R, 7, 0:F], ACT.Copy).then_inc(sem("wattT_copied"), 1)
            lin_bias(1)
            ssp(Z)
            act.wait_ge(sem("xj_in_psum"), 1)
            for h in range(2):
                nc.scalar.activation(XJn[:, HALF * h:HALF * h + 12, :].rearrange("p (a b) f -> p a b f", a=3),
                                     PS[0:P, 0:3, :].rearrange("p a (b h f) -> p a b h f", h=2, f=F)[:, :, :, h, :],
                                     ACT.Copy).then_inc(sem("xj_part"), 1)
                nc.scalar.activation(XJn[:, HALF * h + 12, :], PS[0:P, 3, F * h:F * h + F], ACT.Copy).then_inc(sem("xj_part"), 1)
            act.wait_ge(sem("xj_part"), 4)
            act.dma_start(xj_dram.rearrange("(t p) f -> p t f", p=P), XJn[:, 0:NT, :]).then_inc(sem("xj_stored"), 16)
            act.wait_ge(sem("wblk_zeroed"), 1)
            act.wait_ge(sem("wattT_copied"), 1)
            for j in range(G):
                act.dma_start(Wblk[R * j:R * j + R, F * j:F * j + F], WattT).then_inc(sem("wblk_ready"), 16)
            for u in range(2):
                load_features(act, u, u, False)
            lin_bias(0)
            ssp(Z)

            def edge_group(g, u, first):
                act.wait_ge(sem("fT_in_psum"), g + 1)
                act.wait_ge(sem("g_in_psum"), g)
                nc.scalar.activation(fT, PS[:, 4, 0:EP], ACT.Copy).then_inc(sem("fT_copied"), 1)
                act.wait_ge(sem("comb_in_psum"), g + 1)
                if not first:
                    for a in range(ACCS):
                        act.wait_ge(sem(f"sum_added{a}"), 16 * TURNS * (g - 1))
                nc.scalar.activation(cm[u], PS[:, 6, :], ACT.Copy).then_inc(sem("combined"), 1)

            for u in range(2):
                edge_group(u, u, True)
            with act.Fori(1, NG // 2) as k:
                for u in range(2):
                    edge_group(2 * k + u, u, False)

            for k in range(4):
                for a in range(5):
                    n = 5 * k + a
                    if k < 3:
                        act.wait_ge(sem("block_biased"), n + 1)
                        nc.scalar.activation(cols(LG, a), cols(Z, a), ACT.Abs).then_inc(sem("block_abs"), 1)
                    else:
                        act.wait_ge(sem("residual_added"), 10 + a + 1)
                        nc.scalar.activation(cols(LG, a), cols(M, a), ACT.Abs).then_inc(sem("block_abs"), 1)
                    act.wait_ge(sem("block_abs"), n + 1)
                    nc.scalar.activation(cols(LG, a), cols(LG, a), ACT.Exp, scale=-1.0).then_inc(sem("block_exp"), 1)
                    act.wait_ge(sem("block_exp"), n + 1)
                    nc.scalar.activation(cols(LG, a), cols(LG, a), ACT.Ln, scale=0.5, bias=halfc[:, :]).then_inc(sem("block_ln"), 1)
            act.wait_ge(sem("y_in_psum"), 1)
            for h in range(2):
                nc.scalar.activation(H[:, HALF * h:HALF * h + 12, :].rearrange("p (a b) f -> p a b f", a=3),
                                     PS[0:P, 0:3, :].rearrange("p a (b h f) -> p a b h f", h=2, f=F)[:, :, :, h, :],
                                     ACT.Copy).then_inc(sem("y_nodes"), 1)
            nc.scalar.activation(H[:, 12, :], PS[0:P, 3, 0:F], ACT.Copy).then_inc(sem("y_nodes"), 1)

            def ln_act(k):
                act.wait_ge(sem("ln_centered"), k + 1)
                nc.scalar.activation(lnsq, H, ACT.Square).then_inc(sem("ln_squared"), 1)
                act.wait_ge(sem("ln_var"), k + 1)
                nc.scalar.activation(lnvar, lnvar, ACT.Sqrt).then_inc(sem("ln_std"), 1)

            ln_act(0)
            load_exp_ln()

            for l in range(2):
                act.wait_ge(sem("hT_cleared"), 2 * (l + 1))
                for b in range(7):
                    n = min(4, NT - 4 * b)
                    act.wait_ge(sem("h_block"), 7 * l + b + 1)
                    nc.scalar.activation(hT[0:F, 4 * b * P:(4 * b + n) * P], PS[0:F, b, 0:n * P], ACT.Copy
                                         ).then_inc(sem("hT_copied"), 1)
                for c in range(QKN):
                    act.wait_ge(sem("qk_in_psum"), 2 * QKN * l + 2 * c + 1)
                    nc.scalar.activation(qT[:, c * QC:(c + 1) * QC], qk_bank(2 * c), ACT.Copy, scale=0.125).then_inc(sem("q_copied"), 1)

                def values(b):
                    n = min(2, NT - 2 * b)
                    act.wait_ge(sem("v_in_psum"), 13 * l + b + 1)
                    pv = PS[0:P, 6 + b % 2, 0:n * 192].rearrange("p (t c) -> p t c", t=n)
                    for h in range(HEADS):
                        nc.scalar.activation(V[:, 2 * b:2 * b + n, h, 0:F], pv[:, :, F * h:F * h + F], ACT.Copy).then_inc(sem("v_copied"), 1)
                    nc.scalar.activation(SK[:, 2 * b:2 * b + n, :], pv[:, :, 128:192], ACT.Copy).then_inc(sem("v_copied"), 1)

                def logs(c, i):
                    n = c * NT + i
                    act.wait_ge(sem(f"count_loaded{i % RING}"), 16 * (NT // RING) * c + 16 * (i // RING + 1))
                    if not (isinstance(n, int) and n < RING):
                        act.wait_ge(sem("masked"), n - RING + 1)
                    nc.scalar.activation(Lb[i % RING], Cb[i % RING], ACT.Abs).then_inc(sem("magnitude"), 1)
                    act.wait_ge(sem("magnitude"), n + 1)
                    nc.scalar.activation(Lb[i % RING], Lb[i % RING], ACT.Ln, bias=halfc[0:P, :]).then_inc(sem("logged"), 1)

                def exps(c, b, i):
                    if isinstance(c, int) and c == NC - 1:
                        if i % 2:
                            act.wait_ge(sem("shifted_by_vector"), l * (NT // 2) + i // 2 + 1)
                        else:
                            act.wait_ge(sem("shifted"), (l + 1) * (ATT - NT // 2) - (NT + 1) // 2 + i // 2 + 1)
                    else:
                        act.wait_ge(sem("shifted"), l * (ATT - NT // 2) + c * NT + i + 1)
                    nc.scalar.activation(Tt[:, b, i], Tt[:, b, i], ACT.Exp).then_inc(sem("weighed"), 1)

                def copy_q(c):
                    if not (isinstance(c, int) and l == 0 and c == 0):
                        act.wait_ge(sem("scores_in_psum"), l * ATT + c * NT)
                    for h in range(HEADS):
                        nc.scalar.activation(qc[F * h:F * h + F, h * D:h * D + D], qT[F * h:F * h + F, bass.ds(c * D, D)], ACT.Copy
                                             ).then_inc(sem("qc_ready"), 1)

                def stage(c, b, first, last):
                    if not last and l == 0:
                        for i in range(LOG_LAG):
                            logs(c, i)
                    if not first:
                        act.wait_ge(sem("max_in_psum"), l * NC + c)
                        nc.scalar.activation(MB, PS[0:P, 7, 0:HEADS * D].rearrange("p (h d) -> p h d", h=HEADS), ACT.Copy).then_inc(sem("max_spread"), 1)
                    for i in range(NT):
                        if not first:
                            exps(c - 1, 1 - b, i)
                        if not last and l == 0 and i + LOG_LAG < NT:
                            logs(c, i + LOG_LAG)
                        if first and i % 2 == 0:
                            values(i // 2)
                    if not last and not (isinstance(c, int) and c == NC - 1):
                        copy_q(c + 1)
                    if not first:
                        act.wait_ge(sem("weighted_sums"), l * ATT + c * NT)
                        for h in range(HEADS):
                            nc.scalar.activation(AO[h][:, bass.ds((c - 1) * D, D)], PS[0:VW, 6, h * D:(h + 1) * D], ACT.Copy
                                                 ).then_inc(sem("attended"), 1)

                if l == 0:
                    act.sem_inc(sem("attended"), 2)
                act.wait_ge(sem("q_copied"), QKN * (l + 1))
                act.wait_ge(sem("qc_zeroed"), 1)
                copy_q(0)
                stage(0, 0, True, False)
                with act.Fori(0, NC // 2 - 1) as k:
                    stage(2 * k + 1, 1, False, False)
                    stage(2 * k + 2, 0, False, False)
                stage(NC - 2, 1, False, False)
                stage(NC - 1, 0, False, False)
                stage(NC, 1, False, True)
                for b in range(9):
                    n = min(3, NT - 3 * b)
                    act.wait_ge(sem("att_block"), 9 * l + b + 1)
                    nc.scalar.activation(NDn[:, 3 * b:3 * b + n].rearrange("p t h c -> p (t h c)"), PS[0:P, b % 6, 0:n * HEADS * VW], ACT.Copy
                                         ).then_inc(sem("att_copied"), 1)
            ln_act(1)

        @block.vector
        def _(dve):
            ssp_n, lin_n = [0], [0]

            def ssp(z, dest):
                ssp_n[0] += 1
                dve.wait_ge(sem("ssp_ln"), ssp_n[0])
                nc.vector.scalar_tensor_tensor(dest, z, 0.0, LG, ALU.max, ALU.add).then_inc(sem("ssp_done"), 1)

            chain = [0]

            def link(ins):
                chain[0] += 1
                ins.then_inc(sem("vector_chain"), 1)
                dve.wait_ge(sem("vector_chain"), chain[0])

            nc.vector.memset(qc, 0.0).then_inc(sem("qc_zeroed"), 1)
            nc.vector.memset(halfc[:, :], 0.5).then_inc(sem("half_set"), 1)
            nc.vector.memset(X[:, HALF - 1, 1, :], 0.0).then_inc(sem("pad_zeroed"), 1)
            dve.wait_ge(sem("ident_ready"), 1)
            nc.vector.tensor_copy(identh[:, :], ident[:, :]).then_inc(sem("ident16_ready"), 1)
            dve.wait_ge(sem("trash_iota"), 2)
            nc.vector.tensor_copy(trash, trash_i).then_inc(sem("trash_ready"), 1)
            dve.wait_ge(sem("trash_ready"), 1)
            dve.wait_ge(sem("edges_loaded"), 64)

            def stage_targets(g, u):
                nc.vector.tensor_copy(dcur[u], dst_i[:, bass.ds(g * G, G)]).then_inc(sem("targets_staged"), 1)

            def stage(g):
                sl = bass.ds(g * G, G)
                nc.vector.tensor_copy(srcf, src_i[:, sl]).then_inc(sem("keys_copied"), 1)
                nc.vector.tensor_copy(dstf, dst_i[:, sl]).then_inc(sem("keys_copied"), 1)
                nc.vector.tensor_scalar(srch, src_i[:, sl], float(-(N // 2)), None, ALU.add).then_inc(sem("keys_copied"), 1)
                nc.vector.tensor_scalar(dsth, dst_i[:, sl], float(-(N // 2)), None, ALU.add).then_inc(sem("keys_copied"), 1)
                dve.wait_ge(sem("keys_copied"), 4 * g + 4)
                dve.sem_inc(sem("staged"), 1)

            def compute(g, u, k, first, last):
                if not last:
                    stage_targets(g + 1, 1 - u)
                dve.wait_ge(sem("keys_in_psum"), g + 1)
                dve.wait_ge(sem("comb_in_psum"), g)
                for b in range(2):
                    q = slice(4 * b, 4 * b + 4)
                    for key, sel, bank in ((srch, SelS, b), (dsth, SelD, 2 + b)):
                        nc.vector.tensor_tensor(sel[:, q, :], PS[:, bank, 0:4 * EP].rearrange("p (a b) -> p a b", a=4),
                                                key[:, q].unsqueeze(2).to_broadcast([EP, 4, EP]), ALU.is_equal
                                                ).then_inc(sem("matched"), 1)
                dve.wait_ge(sem("matched"), 4 * g + 4)
                nc.vector.tensor_tensor(SelP, SelS, SelD, ALU.mult).then_inc(sem("pairs"), 1)
                lowb = low.unsqueeze(1).to_broadcast([EP, G, EP])
                nc.vector.tensor_tensor(tmpS, SelS, lowb, ALU.mult).then_inc(sem("before_s"), 1)
                dve.wait_ge(sem("pairs"), g + 1)
                nc.vector.tensor_tensor(tmpP, SelP, lowb, ALU.mult).then_inc(sem("before_p"), 1)
                if not first:
                    dve.wait_ge(sem("count_added"), 16 * G * (g - 1))
                    for a in range(ACCS):
                        dve.wait_ge(sem(f"sum_added{a}"), 16 * TURNS * (g - 1))
                nc.vector.tensor_reduce(cnt[u], SelP, AX, ALU.add).then_inc(sem("counted"), 1)
                dve.wait_ge(sem("before_s"), g + 1)
                nc.vector.tensor_reduce(preS, tmpS, AX, ALU.add).then_inc(sem("earlier"), 1)
                dve.wait_ge(sem("before_p"), g + 1)
                nc.vector.tensor_reduce(preP, tmpP, AX, ALU.add).then_inc(sem("earlier"), 1)
                nc.vector.scalar_tensor_tensor(base, srcf, float(ND), dstf, ALU.mult, ALU.add).then_inc(sem("cells"), 1)
                nc.vector.tensor_scalar(tS, srcf, -1.0, trash[:, 0:1], ALU.mult, ALU.add).then_inc(sem("to_trash"), 1)
                dve.wait_ge(sem("cells"), g + 1)
                nc.vector.tensor_scalar(tC, base, -1.0, trash[:, 1:2], ALU.mult, ALU.add).then_inc(sem("to_trash"), 1)
                dve.wait_ge(sem("to_trash"), 2 * g + 2)
                dve.wait_ge(sem("earlier"), 2 * g + 2)
                nc.vector.scalar_tensor_tensor(tS, preS, 0.0, tS, ALU.is_gt, ALU.mult).then_inc(sem("moved"), 1)
                nc.vector.scalar_tensor_tensor(tC, preP, 0.0, tC, ALU.is_gt, ALU.mult).then_inc(sem("moved"), 1)
                dve.wait_ge(sem("moved"), 2 * g + 2)
                nc.vector.tensor_tensor(sidx[u], tS, srcf, ALU.add).then_inc(sem("index_parts"), 1)
                nc.vector.tensor_tensor(cidx[u], tC, base, ALU.add).then_inc(sem("index_parts"), 1)
                dve.wait_ge(sem("counted"), g + 1)
                dve.wait_ge(sem("index_parts"), 2 * g + 2)
                dve.sem_inc(sem("indexed"), 1)
                if not last:
                    stage(g + 1)
                dve.wait_ge(sem(f"gathered{u}"), 16 * G * (k + 1))
                dve.wait_ge(sem("g_in_psum"), g + 1)
                nc.vector.tensor_tensor(msg.rearrange("p a b -> p (a b)"), gx[u], PS[:, 5, :], ALU.mult).then_inc(sem("messages"), 1)

            stage_targets(0, 0)
            stage(0)
            ssp(xT2, XA)
            ssp(Z, XJ)
            ssp(Z, M)
            dve.wait_ge(sem("low_ready"), 1)
            for u in range(2):
                compute(u, u, 0, True, False)
            with dve.Fori(1, NG // 2 - 1) as k:
                for u in range(2):
                    compute(2 * k + u, u, k, False, False)
            for u in range(2):
                compute(NG - 2 + u, u, NG // 2 - 1, False, u == 1)

            nc.vector.memset(AGG[:, HALF - 1, 1, :], 0.0).then_inc(sem("pad_zeroed"), 1)
            dve.wait_ge(sem("sums_loaded0"), 16)
            for u in range(1, ACCS - 1):
                dve.wait_ge(sem(f"sums_loaded{u}"), 16)
                link(nc.vector.tensor_tensor(ACC[0], ACC[0], ACC[u], ALU.add))
            dve.wait_ge(sem(f"sums_loaded{ACCS - 1}"), 16)
            nc.vector.tensor_tensor(AGG[:, :, 0, :], ACC[0][:, 0:HALF, :], ACC[ACCS - 1][:, 0:HALF, :], ALU.add).then_inc(sem("pad_zeroed"), 1)
            nc.vector.tensor_tensor(AGG[:, 0:NT - HALF, 1, :], ACC[0][:, HALF:NT, :], ACC[ACCS - 1][:, HALF:NT, :], ALU.add).then_inc(sem("pad_zeroed"), 1)
            dve.wait_ge(sem("pad_zeroed"), 4)
            dve.sem_inc(sem("sums_ready"), 1)
            dve.wait_ge(sem("sum_blocks"), 1)
            nc.vector.tensor_tensor(M[:, 0:1500].rearrange("p (a b) -> p a b", a=3), M[:, 0:1500].rearrange("p (a b) -> p a b", a=3),
                                    pairs[0], ALU.add).then_inc(sem("m_part"), 1)
            nc.vector.tensor_tensor(M[:, 1500:HC], M[:, 1500:HC], PS[:, 3, 0:P], ALU.add).then_inc(sem("m_part"), 1)
            dve.wait_ge(sem("m_part"), 2)
            dve.sem_inc(sem("m_updated"), 1)
            for k in range(3):
                for a in range(5):
                    dve.wait_ge(sem("product_done"), 10 * k + a + 1)
                    nc.vector.tensor_scalar(cols(Z, a), product(2 * k, a), BC[:, 4 + k:5 + k], None, ALU.add
                                            ).then_inc(sem("block_biased"), 1)
                for a in range(5):
                    dve.wait_ge(sem("block_ln"), 5 * k + a + 1)
                    nc.vector.scalar_tensor_tensor(cols(XA, a), cols(Z, a), 0.0, cols(LG, a), ALU.max, ALU.add).then_inc(sem("block_ssp"), 1)
                for a in range(5):
                    dve.wait_ge(sem("product_done"), 10 * k + 5 + a + 1)
                    nc.vector.scalar_tensor_tensor(cols(M, a), product(2 * k + 1, a), BC[:, 7 + k:8 + k], cols(M, a), ALU.add, ALU.add
                                                   ).then_inc(sem("residual_added"), 1)
            for a in range(5):
                dve.wait_ge(sem("block_ln"), 15 + a + 1)
                nc.vector.scalar_tensor_tensor(cols(XA, a), cols(M, a), 0.0, cols(LG, a), ALU.max, ALU.add).then_inc(sem("block_ssp"), 1)
            for a in range(5):
                dve.wait_ge(sem("product_done"), 30 + a + 1)
                nc.vector.scalar_tensor_tensor(cols(Z, a), cols(xT2, a), BC[:, 3:4], product(6, a), ALU.mult, ALU.add
                                               ).then_inc(sem("gated"), 1)
            for a in range(5):
                dve.wait_ge(sem("gated"), a + 1)
                nc.vector.scalar_tensor_tensor(cols(Z, a), cols(Z, a), BC[:, 2:3], cols(xT2, a), ALU.add, ALU.add
                                               ).then_inc(sem("y_ready"), 1)

            def layernorm(k, dest):
                link(nc.vector.tensor_reduce(lnsum, H, AX, ALU.add))
                link(nc.vector.tensor_scalar(lnsum, lnsum, 1.0 / F, None, ALU.mult))
                nc.vector.tensor_tensor(H, H, lnsum.unsqueeze(2).to_broadcast([P, NT, F]), ALU.subtract).then_inc(sem("ln_centered"), 1)
                dve.wait_ge(sem("ln_squared"), k + 1)
                link(nc.vector.tensor_reduce(lnvar, lnsq, AX, ALU.add))
                nc.vector.tensor_scalar(lnvar, lnvar, 1.0 / F, 1e-5, ALU.mult, ALU.add).then_inc(sem("ln_var"), 1)
                dve.wait_ge(sem("ln_std"), k + 1)
                link(nc.vector.reciprocal(lnvar, lnvar))
                return nc.vector.tensor_tensor(dest, H, lnvar.unsqueeze(2).to_broadcast([P, NT, F]), ALU.mult)

            dve.wait_ge(sem("y_nodes"), 3)
            layernorm(0, X1).then_inc(sem("h_ready"), 1)

            for l in range(2):
                nc.vector.memset(hTt[0:F, N:ND], 0.0).then_inc(sem("hT_cleared"), 1)
                if l == 0:
                    for h in range(HEADS):
                        nc.vector.memset(V[:, :, h, F:F + 1], 1.0).then_inc(sem("ones_set"), 1)
                for c in range(QKN):
                    dve.wait_ge(sem("qk_in_psum"), 2 * QKN * l + 2 * c + 2)
                    nc.vector.tensor_copy(kT[:, c * QC:(c + 1) * QC], qk_bank(2 * c + 1)).then_inc(sem("k_copied"), 1)

                def log_mask(c, i):
                    dve.wait_ge(sem("logged"), c * NT + i + 1)
                    nc.vector.scalar_tensor_tensor(Cb[i % RING], Cb[i % RING], BIG, Lb[i % RING], ALU.mult, ALU.min
                                                   ).then_inc(sem("masked"), 1)

                def score(c, b, i):
                    n = l * ATT + c * NT + i
                    if l == 0:
                        dve.wait_ge(sem("masked"), n + 1)
                    else:
                        dve.wait_ge(sem(f"count_loaded{i % RING}"), 16 * (NT // RING) * c + 16 * (l * ATT // RING + i // RING + 1))
                    dve.wait_ge(sem("scores_in_psum"), n + 1)
                    nc.vector.tensor_tensor(Tt[:, b, i], score_ring[i % BANKS].rearrange("p (h d) -> p h d", h=HEADS),
                                            Cb[i % RING].unsqueeze(1).to_broadcast([P, HEADS, D]), ALU.add).then_inc(sem("scored"), 1)

                def running(c, b, i):
                    n = l * ATT + c * NT + i
                    dve.wait_ge(sem("scored"), n + 1)
                    if i == 0:
                        nc.vector.tensor_copy(RM, Tt[:, b, 0]).then_inc(sem("max_run"), 1)
                    else:
                        dve.wait_ge(sem("max_run"), n)
                        nc.vector.tensor_tensor(RM, RM, Tt[:, b, i], ALU.max).then_inc(sem("max_run"), 1)

                def column_max(c):
                    dve.wait_ge(sem("max_moved"), l * NC + c + 1)
                    nc.vector.tensor_reduce(mrow, PS[0:MW, 7, 0:BLK * HEADS * P].rearrange("p (a b) -> p a b", b=P), AX, ALU.max
                                            ).then_inc(sem("max_reduced"), 1)
                    dve.wait_ge(sem("max_reduced"), l * NC + c + 1)
                    nc.vector.tensor_scalar(mrow, mrow, FLOOR, None, ALU.max).then_inc(sem("max_ready"), 1)

                def stage_att(c, b, first):
                    for i in range(NT + 2):
                        if i < NT and l == 0:
                            log_mask(c, i)
                        if i == 0 and not first:
                            column_max(c - 1)
                        if i >= 2:
                            score(c, b, i - 2)
                            running(c, b, i - 2)

                stage_att(0, 0, True)
                with dve.Fori(0, NC // 2) as k:
                    stage_att(2 * k + 1, 1, False)
                    stage_att(2 * k + 2, 0, False)
                column_max(NC - 1)
                dve.wait_ge(sem("max_spread"), NC * (l + 1))
                for i in range(1, NT, 2):
                    nc.vector.tensor_tensor(Tt[:, 0, i], Tt[:, 0, i], MB, ALU.subtract).then_inc(sem("shifted_by_vector"), 1)

                dve.wait_ge(sem("att_copied"), 9 * (l + 1))
                link(nc.vector.tensor_scalar(rec, NDn[:, :, :, F], 1e-16, None, ALU.add))
                link(nc.vector.reciprocal(rec, rec))
                link(nc.vector.tensor_tensor(att, NDn.rearrange("p t h c -> p (t h) c")[:, :, 0:F],
                                             rec.rearrange("p t h -> p (t h)").unsqueeze(2).to_broadcast([P, NT * HEADS, F]), ALU.mult))
                link(nc.vector.tensor_tensor(H, att4[:, :, 0, :], att4[:, :, 1, :], ALU.add))
                ins = nc.vector.scalar_tensor_tensor(H, H, 0.5, SK, ALU.mult, ALU.add)
                if l == 0:
                    link(ins)
                    dve.sem_inc(sem("h_ready"), 1)
                else:
                    link(ins)
            link(nc.vector.tensor_tensor(H, H, X1, ALU.add))
            layernorm(1, H).then_inc(sem("result_ready"), 1)

        @block.tensor
        def _(pe):
            lin_n = [0]

            def lin(w, v):
                pe.wait_ge(sem("lin_used"), lin_n[0])
                lin_n[0] += 1
                for a in range(5):
                    ins = nc.tensor.matmul(PS[:, a, 0:LC], BD[:, w, :], v[:, a * LC:(a + 1) * LC], start=True, stop=True)
                ins.then_inc(sem("lin_done"), 1)

            pe.wait_ge(sem("ident_ready"), 1)
            pe.wait_ge(sem("x_loaded"), 32)
            pe.wait_ge(sem("pad_zeroed"), 1)

            def to_features(a, name):
                for j in range(HALF):
                    ins = nc.tensor.transpose(block_at[j], a[:, j, :, :].rearrange("p h f -> p (h f)"), ident[0:P, 0:P])
                ins.then_inc(sem(name), 1)

            def to_nodes(a, name):
                for j in range(HALF):
                    ins = nc.tensor.transpose(node_at[j], a[:, j * P:(j + 1) * P], ident[:, :])
                ins.then_inc(sem(name), 1)

            to_features(X, "x_blocks")
            pe.wait_ge(sem("weights_loaded"), 16 * 22)
            for i in range(9):
                ins = nc.tensor.transpose(PS[:, 4 + i // 4, (i % 4) * 128:(i % 4 + 1) * 128], BDraw[:, i, :], ident[:, :])
            ins.then_inc(sem("bd_in_psum"), 1)
            pe.wait_ge(sem("watt_loaded"), 16)
            nc.tensor.transpose(PS[0:R, 7, 0:F], Watt, ident[0:F, 0:F]).then_inc(sem("watt_in_psum"), 1)
            pe.wait_ge(sem("bd_ready"), 2)
            pe.wait_ge(sem("ssp_done"), 1)
            lin(1, XA)
            pe.wait_ge(sem("ssp_done"), 2)
            to_nodes(XJ, "xj_in_psum")
            pe.wait_ge(sem("xj_part"), 4)
            lin(0, XA)

            pe.wait_ge(sem("lin_used"), 2)
            pe.wait_ge(sem("ident16_ready"), 1)
            pe.wait_ge(sem("wattT_copied"), 1)

            def edge_group(g, u, k):
                pe.wait_ge(sem("staged"), g + 1)
                pe.wait_ge(sem("matched"), 4 * g)
                for key, bank in ((srch, 0), (dsth, 2)):
                    for s in range(G):
                        ins = nc.tensor.matmul(PS[:, bank + s // 4, (s % 4) * EP:(s % 4 + 1) * EP],
                                               key[:, s:s + 1].to_broadcast([EP, EP]), identh[:, :], start=True, stop=True)
                ins.then_inc(sem("keys_in_psum"), 1)
                pe.wait_ge(sem(f"f_loaded{u}"), 32 * (k + 1))
                pe.wait_ge(sem("fT_copied"), g)
                nc.tensor.transpose(PS[:, 4, 0:EP], f8[u], ident[:, :]).then_inc(sem("fT_in_psum"), 1)
                pe.wait_ge(sem("fT_copied"), g + 1)
                pe.wait_ge(sem("messages"), g)
                nc.tensor.matmul(PS[:, 5, :], fT, Wblk, start=True, stop=True).then_inc(sem("g_in_psum"), 1)
                pe.wait_ge(sem("matched"), 4 * g + 4)
                pe.wait_ge(sem("messages"), g + 1)
                pe.wait_ge(sem("combined"), g)
                for s in range(G):
                    ins = nc.tensor.matmul(PS[:, 6, s * F:(s + 1) * F], SelS[:, s, :], msg[:, s, :], start=True, stop=True)
                ins.then_inc(sem("comb_in_psum"), 1)

            pe.wait_ge(sem("wblk_ready"), 16 * G)
            for u in range(2):
                edge_group(u, u, 0)
            with pe.Fori(1, NG // 2) as k:
                for u in range(2):
                    edge_group(2 * k + u, u, k)

            pe.wait_ge(sem("sums_ready"), 1)
            to_features(AGG, "sum_blocks")
            pe.wait_ge(sem("m_updated"), 1)
            for k in range(3):
                for a in range(5):
                    if k:
                        pe.wait_ge(sem("residual_added"), 5 * (k - 1) + a + 1)
                    nc.tensor.matmul(product(2 * k, a), BD[:, 3 + k, :], cols(M, a), start=True, stop=True).then_inc(sem("product_done"), 1)
                for a in range(5):
                    pe.wait_ge(sem("block_ssp"), 5 * k + a + 1)
                    nc.tensor.matmul(product(2 * k + 1, a), BD[:, 6 + k, :], cols(XA, a), start=True, stop=True).then_inc(sem("product_done"), 1)
            for a in range(5):
                pe.wait_ge(sem("block_ssp"), 15 + a + 1)
                nc.tensor.matmul(product(6, a), BD[:, 2, :], cols(XA, a), start=True, stop=True).then_inc(sem("product_done"), 1)
            pe.wait_ge(sem("y_ready"), 5)
            to_nodes(Z, "y_in_psum")

            pe.wait_ge(sem("layer_weights"), 16 * 16)
            for l in range(2):
                Hin = X1 if l == 0 else H
                pe.wait_ge(sem("h_ready"), l + 1)
                for b in range(7):
                    n = min(4, NT - 4 * b)
                    for t in range(n):
                        ins = nc.tensor.transpose(PS[0:F, b, t * P:(t + 1) * P], Hin[:, 4 * b + t, :], ident[0:P, 0:P])
                    ins.then_inc(sem("h_block"), 1)
                pe.wait_ge(sem("hT_copied"), 7 * (l + 1))

                for c in range(QKN):
                    for j, (w, copied) in enumerate(((wq_(l), "q_copied"), (wk_(l), "k_copied"))):
                        if c >= BANKS // 2:
                            pe.wait_ge(sem(copied), QKN * l + c - BANKS // 2 + 1)
                        nc.tensor.matmul(qk_bank(2 * c + j), w, hT[:, c * QC:(c + 1) * QC], start=True, stop=True
                                         ).then_inc(sem("qk_in_psum"), 1)
                pe.wait_ge(sem("q_copied"), QKN * (l + 1))
                pe.wait_ge(sem("k_copied"), QKN * (l + 1))

                def values(b):
                    v = 13 * l + b
                    if b >= 2:
                        pe.wait_ge(sem("v_copied"), 3 * (v - 1))
                    for t in range(2 * b, min(2 * b + 2, NT)):
                        ins = nc.tensor.matmul(PS[0:P, 6 + b % 2, t % 2 * 192:(t % 2 + 1) * 192], hT[:, t * P:(t + 1) * P], wv_(l),
                                               start=True, stop=True)
                    ins.then_inc(sem("v_in_psum"), 1)

                def scores(c, i):
                    n = l * ATT + c * NT + i
                    if not (isinstance(n, int) and n < BANKS):
                        pe.wait_ge(sem("scored"), n if i == 0 else n - BANKS + 1)
                    nc.tensor.matmul(score_ring[i % BANKS], kT[:, i * P:(i + 1) * P], qc, start=True, stop=True
                                     ).then_inc(sem("scores_in_psum"), 1)

                def weighted(c, b, i):
                    n = l * ATT + c * NT + i
                    pe.wait_ge(sem("weighed"), n + 1)
                    if i == 0:
                        pe.wait_ge(sem("attended"), 2 * (l * NC + c + 1))
                    for h in range(HEADS):
                        ins = nc.tensor.matmul(PS[0:VW, 6, h * D:(h + 1) * D], V[:, i, h, :], Tt[:, b, i, h, :],
                                               start=i == 0 and h == 0, stop=i == NT - 1, skip_group_check=True)
                    ins.then_inc(sem("weighted_sums"), 1)

                def move_max(c):
                    pe.wait_ge(sem("max_run"), l * ATT + (c + 1) * NT)
                    for q in range(BLK * HEADS):
                        ins = nc.tensor.transpose(PS[0:MW, 7, q * P:(q + 1) * P], Rt[0:P, q * MW:(q + 1) * MW], ident[0:P, 0:P])
                    ins.then_inc(sem("max_moved"), 1)

                def spread_max(c):
                    pe.wait_ge(sem("max_ready"), l * NC + c + 1)
                    for q in range(BLK * HEADS):
                        ins = nc.tensor.matmul(PS[0:P, 7, q * MW:(q + 1) * MW], mrow[:, q:q + 1].to_broadcast([MW, P]),
                                               ident[0:MW, 0:MW], start=True, stop=True)
                    ins.then_inc(sem("max_in_psum"), 1)

                def stage_att(c, b, first, last):
                    if not last:
                        pe.wait_ge(sem("qc_ready"), HEADS * (l * NC + c + 1))
                    for i in range(LAG):
                        if not last:
                            scores(c, i)
                        if not first and i == 0:
                            move_max(c - 1)
                        if not first and i == 1:
                            spread_max(c - 1)
                    for i in range(NT):
                        if not last and i + LAG < NT:
                            scores(c, i + LAG)
                        if first and i % 2 == 0:
                            values(i // 2)
                        if not first:
                            weighted(c - 1, 1 - b, i)

                stage_att(0, 0, True, False)
                pe.wait_ge(sem("v_copied"), 39 * (l + 1))
                pe.wait_ge(sem("ones_set"), 2)
                with pe.Fori(0, NC // 2) as k:
                    stage_att(2 * k + 1, 1, False, False)
                    stage_att(2 * k + 2, 0, False, False)
                stage_att(NC, 1, False, True)
                pe.wait_ge(sem("attended"), 2 * (NC * (l + 1) + 1))
                for b in range(9):
                    n = min(3, NT - 3 * b)
                    if b >= 6:
                        pe.wait_ge(sem("att_copied"), 9 * l + b - 5)
                    for t in range(3 * b, 3 * b + n):
                        for h in range(HEADS):
                            o = (2 * (t - 3 * b) + h) * VW
                            ins = nc.tensor.transpose(PS[0:P, b % 6, o:o + VW], AO[h][:, t * P:(t + 1) * P], ident[0:VW, 0:VW])
                    ins.then_inc(sem("att_block"), 1)



_INS = ['x', 'src', 'dst', 'edge_attr_16', 'L0_gnn_W_att', 'L0_gnn_W_i', 'L0_gnn_b_i', 'L0_gnn_W_j', 'L0_gnn_b_j', 'L0_gnn_W_v', 'L0_gnn_b_v', 'L0_gnn_res_dense_W', 'L0_gnn_res_dense_b', 'L0_gnn_res_res_W', 'L0_gnn_res_res_b', 'L0_gnn_gate', 'L1_gnn_l1_wq', 'L1_gnn_l1_bq', 'L1_gnn_l1_wk', 'L1_gnn_l1_bk', 'L1_gnn_l1_wv', 'L1_gnn_l1_bv', 'L1_gnn_l1_ws', 'L1_gnn_l1_bs', 'L1_gnn_l2_wq', 'L1_gnn_l2_bq', 'L1_gnn_l2_wk', 'L1_gnn_l2_bk', 'L1_gnn_l2_wv', 'L1_gnn_l2_bv', 'L1_gnn_l2_ws', 'L1_gnn_l2_bs']
_OUTS = [((3125, 64), 'float32')]


def kernel(**inputs):
    import numpy as _np
    import concourse.bacc as _bacc
    from concourse import mybir as _mybir
    from concourse.bass_utils import run_bass_kernel_spmd as _run

    nc = _bacc.Bacc("TRN2", target_bir_lowering=False, num_devices=1)
    arrays, args = {}, []
    for name in _INS:
        a = _np.ascontiguousarray(inputs[name])
        arrays[f"in_{name}_dram"] = a
        args.append(nc.dram_tensor(f"in_{name}_dram", a.shape, _mybir.dt.from_np(a.dtype), kind="ExternalInput").ap())
    for i, (shape, dtype) in enumerate(_OUTS):
        dt = _mybir.dt.from_np(_np.dtype(dtype))
        args.append(nc.dram_tensor(f"out_{i}_dram", shape, dt, kind="ExternalOutput").ap())
    build(nc, *args)
    r = _run(nc, [arrays], core_ids=[0])
    return r.results[0]["out_0_dram"]
```
